# Optimizing a Trainium2 kernel written in Bass

```python
import numpy as np
import jax
import jax.numpy as jnp

def _softmax(x, axis=-1):
    return jax.nn.softmax(x, axis=axis)
def _gelu(x):
    return jax.nn.gelu(x, approximate=True)
def _silu(x):
    return jax.nn.silu(x)
def _sigmoid(x):
    return jax.nn.sigmoid(x)
def _layernorm(x, axis=-1, eps=1e-5):
    m = jnp.mean(x, axis=axis, keepdims=True)
    v = jnp.var(x, axis=axis, keepdims=True)
    return (x - m) / jnp.sqrt(v + eps)
def _scatter_add(tgt, idx, src, axis=0):
    return tgt.at[idx].add(src)
def _segment_sum(src, seg, n):
    return jax.ops.segment_sum(src, seg, n)

kernel_name = 'mk_conv_preact_d2_conv_nchw512_25efb1'

def setup_inputs(seed: int = 0):
    np.random.seed(seed)
    _w = jnp.asarray
    def _rec_inputs():
        import jax
        import jax.numpy as jnp
        _gk = jax.random.key(seed)
        x = -0.0001546 + 1 * jax.random.normal(jax.random.fold_in(_gk, 1), (2048, 512, 8, 8), jnp.float32)
        return x
    x = _rec_inputs()
    def _L0_conv_setup():
        import jax, jax.numpy as jnp
        import numpy as np
        _TERMS = [(0, 0, 0, 1), (0, 1, 1, 1), (0, 2, 2, 1), (0, 3, 3, 1), (0, 4, 4, -1), (0, 5, 5, -1), (0, 6, 6, -1), (0, 7, 7, -1), (1, 0, 1, 1), (1, 1, 0, 1), (1, 2, 4, -1), (1, 3, 5, 1), (1, 4, 2, 1), (1, 5, 3, -1), (1, 6, 7, -1), (1, 7, 6, -1), (2, 0, 2, 1), (2, 1, 4, 1), (2, 2, 0, 1), (2, 3, 6, -1), (2, 4, 1, -1), (2, 5, 7, 1), (2, 6, 3, 1), (2, 7, 5, -1), (3, 0, 3, 1), (3, 1, 5, -1), (3, 2, 6, 1), (3, 3, 0, 1), (3, 4, 7, -1), (3, 5, 1, -1), (3, 6, 2, -1), (3, 7, 4, 1), (4, 0, 4, 1), (4, 1, 2, 1), (4, 2, 1, -1), (4, 3, 7, 1), (4, 4, 0, 1), (4, 5, 6, -1), (4, 6, 5, 1), (4, 7, 3, -1), (5, 0, 5, 1), (5, 1, 3, -1), (5, 2, 7, 1), (5, 3, 1, 1), (5, 4, 6, 1), (5, 5, 0, 1), (5, 6, 4, -1), (5, 7, 2, -1), (6, 0, 6, 1), (6, 1, 7, -1), (6, 2, 3, -1), (6, 3, 2, 1), (6, 4, 5, -1), (6, 5, 4, 1), (6, 6, 0, 1), (6, 7, 1, 1), (7, 0, 7, 1), (7, 1, 6, 1), (7, 2, 5, -1), (7, 3, 4, 1), (7, 4, 3, 1), (7, 5, 2, -1), (7, 6, 1, 1), (7, 7, 0, 1)]

        def _clifford_table():
            T = np.zeros((8, 8, 8), dtype=np.float32)
            for k, p, q, s in _TERMS:
                T[k, p, q] = s
            return jnp.asarray(T)
        _T = _clifford_table()
        key = jax.random.key(seed)
        k1, k2 = jax.random.split(key)
        C_in, C_out = (8, 8)
        x = jax.random.normal(k1, (4096, 512, C_in, 8), dtype=jnp.float32)
        weight = jax.random.normal(k2, (C_out, C_in, 8), dtype=jnp.float32) * C_in ** (-0.5)
        bias = jnp.zeros((C_out, 8), dtype=jnp.float32)
        return {'x': x, 'weight': weight, 'bias': bias}
    _L0_conv_all = _L0_conv_setup()
    _L0_conv_in = {k: v for k, v in _L0_conv_all.items() if k in ('weight', 'bias', )}
    del _L0_conv_all

    def _L1_conv_setup():
        import jax, jax.numpy as jnp
        import numpy as np
        from jax import lax
        EPS = 1e-05
        GROUPS = 16

        def _batchnorm(x, gamma, beta):
            m = jnp.mean(x, axis=(0, 2, 3), keepdims=True)
            v = jnp.mean((x - m) ** 2, axis=(0, 2, 3), keepdims=True)
            xhat = (x - m) * lax.rsqrt(v + EPS)
            return xhat * gamma[None, :, None, None] + beta[None, :, None, None]

        @jax.custom_vjp
        def binary_act(x):
            return jnp.sign(x)

        def _ba_fwd(x):
            return (jnp.sign(x), x)

        def _ba_bwd(x, g):
            return (jnp.clip(2.0 - 2.0 * jnp.abs(x), a_min=0.0) * g,)
        binary_act.defvjp(_ba_fwd, _ba_bwd)

        @jax.custom_vjp
        def binary_weight(w):
            return jnp.sign(w)

        def _bw_fwd(w):
            return (jnp.sign(w), w)

        def _bw_bwd(w, g):
            mask = jnp.logical_or(w >= 1.0, w <= -1.0)
            return (jnp.where(mask, 0.0, g),)
        binary_weight.defvjp(_bw_fwd, _bw_bwd)

        def _weight_scale(w):
            co = w.shape[0]
            wf = w.reshape(co, -1)
            bw = wf - jnp.mean(wf, axis=-1, keepdims=True)
            std = jnp.std(wf - jnp.mean(wf, axis=-1, keepdims=True), axis=-1, ddof=1, keepdims=True)
            bw = bw / std
            sw = jnp.mean(jnp.abs(bw), axis=-1).reshape(co, 1, 1, 1)
            return lax.stop_gradient(sw)
        key = jax.random.key(seed)
        ks = jax.random.split(key, 7)
        N, C, H, W = (64, 512, 32, 32)
        k = 3
        x = jax.random.normal(ks[0], (N, C, H, W), dtype=jnp.float32)
        conv_w = jax.random.normal(ks[1], (C, C // GROUPS, k, k), dtype=jnp.float32) * 0.1
        bn1_gamma = jnp.ones((C,), jnp.float32)
        bn1_beta = jnp.zeros((C,), jnp.float32)
        bn2_gamma = jnp.ones((C,), jnp.float32)
        bn2_beta = jnp.zeros((C,), jnp.float32)
        prelu_a = jnp.full((C,), 0.25, jnp.float32)
        return {'x': x, 'conv_w': conv_w, 'bn1_gamma': bn1_gamma, 'bn1_beta': bn1_beta, 'bn2_gamma': bn2_gamma, 'bn2_beta': bn2_beta, 'prelu_a': prelu_a}
    _L1_conv_all = _L1_conv_setup()
    _L1_conv_in = {k: v for k, v in _L1_conv_all.items() if k in ('conv_w', 'bn1_gamma', 'bn1_beta', 'bn2_gamma', 'bn2_beta', 'prelu_a', )}
    del _L1_conv_all

    return {
        "x": x,
        "L0_conv_weight": _L0_conv_in["weight"],
        "L0_conv_bias": _L0_conv_in["bias"],
        "L1_conv_conv_w": _L1_conv_in["conv_w"],
        "L1_conv_bn1_gamma": _L1_conv_in["bn1_gamma"],
        "L1_conv_bn1_beta": _L1_conv_in["bn1_beta"],
        "L1_conv_bn2_gamma": _L1_conv_in["bn2_gamma"],
        "L1_conv_bn2_beta": _L1_conv_in["bn2_beta"],
        "L1_conv_prelu_a": _L1_conv_in["prelu_a"],
    }

def reference(x, L0_conv_weight, L0_conv_bias, L1_conv_conv_w, L1_conv_bn1_gamma, L1_conv_bn1_beta, L1_conv_bn2_gamma, L1_conv_bn2_beta, L1_conv_prelu_a):
    import jax
    import jax.numpy as jnp
    def _L0_conv_ref(x, weight, bias):
        import jax, jax.numpy as jnp
        import numpy as np
        _TERMS = [(0, 0, 0, 1), (0, 1, 1, 1), (0, 2, 2, 1), (0, 3, 3, 1), (0, 4, 4, -1), (0, 5, 5, -1), (0, 6, 6, -1), (0, 7, 7, -1), (1, 0, 1, 1), (1, 1, 0, 1), (1, 2, 4, -1), (1, 3, 5, 1), (1, 4, 2, 1), (1, 5, 3, -1), (1, 6, 7, -1), (1, 7, 6, -1), (2, 0, 2, 1), (2, 1, 4, 1), (2, 2, 0, 1), (2, 3, 6, -1), (2, 4, 1, -1), (2, 5, 7, 1), (2, 6, 3, 1), (2, 7, 5, -1), (3, 0, 3, 1), (3, 1, 5, -1), (3, 2, 6, 1), (3, 3, 0, 1), (3, 4, 7, -1), (3, 5, 1, -1), (3, 6, 2, -1), (3, 7, 4, 1), (4, 0, 4, 1), (4, 1, 2, 1), (4, 2, 1, -1), (4, 3, 7, 1), (4, 4, 0, 1), (4, 5, 6, -1), (4, 6, 5, 1), (4, 7, 3, -1), (5, 0, 5, 1), (5, 1, 3, -1), (5, 2, 7, 1), (5, 3, 1, 1), (5, 4, 6, 1), (5, 5, 0, 1), (5, 6, 4, -1), (5, 7, 2, -1), (6, 0, 6, 1), (6, 1, 7, -1), (6, 2, 3, -1), (6, 3, 2, 1), (6, 4, 5, -1), (6, 5, 4, 1), (6, 6, 0, 1), (6, 7, 1, 1), (7, 0, 7, 1), (7, 1, 6, 1), (7, 2, 5, -1), (7, 3, 4, 1), (7, 4, 3, 1), (7, 5, 2, -1), (7, 6, 1, 1), (7, 7, 0, 1)]

        def _clifford_table():
            T = np.zeros((8, 8, 8), dtype=np.float32)
            for k, p, q, s in _TERMS:
                T[k, p, q] = s
            return jnp.asarray(T)
        _T = _clifford_table()
        wT = jnp.einsum('kpq,oip->oikq', _T.astype(weight.dtype), weight)
        out = jnp.einsum('oikq,biq->bok', wT, x.reshape(-1, *x.shape[-2:]))
        out = out.reshape(*x.shape[:-2], *out.shape[-2:])
        return out + bias

    def _L1_conv_ref(x, conv_w, bn1_gamma, bn1_beta, bn2_gamma, bn2_beta, prelu_a):
        import jax, jax.numpy as jnp
        import numpy as np
        from jax import lax
        EPS = 1e-05
        GROUPS = 16

        def _batchnorm(x, gamma, beta):
            m = jnp.mean(x, axis=(0, 2, 3), keepdims=True)
            v = jnp.mean((x - m) ** 2, axis=(0, 2, 3), keepdims=True)
            xhat = (x - m) * lax.rsqrt(v + EPS)
            return xhat * gamma[None, :, None, None] + beta[None, :, None, None]

        @jax.custom_vjp
        def binary_act(x):
            return jnp.sign(x)

        def _ba_fwd(x):
            return (jnp.sign(x), x)

        def _ba_bwd(x, g):
            return (jnp.clip(2.0 - 2.0 * jnp.abs(x), a_min=0.0) * g,)
        binary_act.defvjp(_ba_fwd, _ba_bwd)

        @jax.custom_vjp
        def binary_weight(w):
            return jnp.sign(w)

        def _bw_fwd(w):
            return (jnp.sign(w), w)

        def _bw_bwd(w, g):
            mask = jnp.logical_or(w >= 1.0, w <= -1.0)
            return (jnp.where(mask, 0.0, g),)
        binary_weight.defvjp(_bw_fwd, _bw_bwd)

        def _weight_scale(w):
            co = w.shape[0]
            wf = w.reshape(co, -1)
            bw = wf - jnp.mean(wf, axis=-1, keepdims=True)
            std = jnp.std(wf - jnp.mean(wf, axis=-1, keepdims=True), axis=-1, ddof=1, keepdims=True)
            bw = bw / std
            sw = jnp.mean(jnp.abs(bw), axis=-1).reshape(co, 1, 1, 1)
            return lax.stop_gradient(sw)
        res = x
        h = _batchnorm(x, bn1_gamma, bn1_beta)
        h = binary_act(h)
        sw = _weight_scale(conv_w)
        bw = binary_weight(conv_w) * sw
        h = lax.conv_general_dilated(h, bw, window_strides=(1, 1), padding=((1, 1), (1, 1)), feature_group_count=GROUPS, dimension_numbers=('NCHW', 'OIHW', 'NCHW'))
        h = _batchnorm(h, bn2_gamma, bn2_beta)
        h = h + res
        a = prelu_a[None, :, None, None]
        return jnp.where(h > 0, h, a * h)

    def _gn(v, G=32, eps=1e-5):
        B_, C_, H_, W_ = v.shape
        g = v.reshape(B_, G, C_ // G, H_, W_)
        m = jnp.mean(g, axis=(2, 3, 4), keepdims=True)
        s = jnp.var(g, axis=(2, 3, 4), keepdims=True)
        return ((g - m) / jnp.sqrt(s + eps)).reshape(v.shape)

    def _ln_c(v, eps=1e-6):
        m = jnp.mean(v, axis=1, keepdims=True)
        s = jnp.var(v, axis=1, keepdims=True)
        return (v - m) / jnp.sqrt(s + eps)

    def _ln_t(v, eps=1e-5):
        m = jnp.mean(v, axis=-1, keepdims=True)
        s = jnp.var(v, axis=-1, keepdims=True)
        return (v - m) / jnp.sqrt(s + eps)

    def _to_tokens(v):
        B_, C_, H_, W_ = v.shape
        return v.reshape(B_, C_, H_ * W_).transpose(0, 2, 1)
    def _from_tokens(t, like):
        B_, C_, H_, W_ = like.shape
        return t.transpose(0, 2, 1).reshape(B_, C_, H_, W_)

    x = x + _L0_conv_ref(_gn(x), L0_conv_weight, L0_conv_bias)
    x = x + _L1_conv_ref(_gn(x), L1_conv_conv_w, L1_conv_bn1_gamma, L1_conv_bn1_beta, L1_conv_bn2_gamma, L1_conv_bn2_beta, L1_conv_prelu_a)
    return x


_drawn_inputs = setup_inputs


def setup_inputs(seed=0):
    import zlib

    import numpy as np

    out = dict(_drawn_inputs(seed))
    spreads = {'L0_conv_bias': (0.0, 0.1),
     'L1_conv_bn1_gamma': (1.0, 0.598),
     'L1_conv_bn1_beta': (0.0, 0.1),
     'L1_conv_bn2_gamma': (1.0, 0.2),
     'L1_conv_bn2_beta': (0.0, 0.407),
     'L1_conv_prelu_a': (0.25, 0.6)}
    factors = {}
    for name, (base, spread) in spreads.items():
        noise = np.random.default_rng([zlib.crc32(name.encode()), seed]).standard_normal(out[name].shape)
        drawn = base * np.exp(spread * noise) if base else spread * noise
        out[name] = jnp.asarray(drawn.astype(out[name].dtype))
    for name, factor in factors.items():
        out[name] = (out[name] * factor).astype(out[name].dtype)
    return out
```

```python
from contextlib import ExitStack

import numpy as np

import concourse.bass as bass
from concourse import mybir

ALU = mybir.AluOpType
ACT = mybir.ActivationFunctionType
F32 = mybir.dt.float32
F16 = mybir.dt.float16
BF16 = mybir.dt.bfloat16

P = 128
C = 512
S = 64
SIDE = 8
J = C // P
NB = 8
FB = NB * J * S
BANK = 512
BANKS = FB // BANK
PER = NB // BANKS
NS = 3
NS2 = 4
EPS = 1e-5
ST = 6
TAPS = 9
PAD = SIDE + 2
CG = 32
UA, UB = 0, 1


SIGNS = ['++++----', '+++--+--', '+-+++--+', '+--++-+-', '+-+-++-+', '++---+++', '+++-+-+-', '++-++-++']


def clifford_terms():
    bits = [0, 1, 2, 4, 3, 5, 6, 7]
    table = np.zeros((8, 8, 8), np.float32)
    for k in range(8):
        for q in range(8):
            table[k, bits.index(bits[k] ^ bits[q]), q] = 1.0 if SIGNS[k][q] == "+" else -1.0
    return table


def two_layer_kernel(nc, x, w0, b0, conv_w, g1, be1, g2, be2, prelu_a, ident_in, gavg_in, clif_in, out):
    N = x.shape[0]
    B = N // NB
    HEAD, TAIL = 4, {NS: 3, NS2: 4}
    assert B * NB == N and all(B > HEAD + t and (B - HEAD - t) % slots == 0 for slots, t in TAIL.items())

    xb = x.rearrange("(b n) (q j) h w -> b q n (j h w)", n=NB, j=J)
    ob = out.rearrange("(b n) (q j) h w -> b q n (j h w)", n=NB, j=J)
    y_len, h_len = C * NB * S, C * NB * S // 2
    y_dram = nc.dram_tensor("y_scratch", [B, y_len], F32).ap()
    h_dram = nc.dram_tensor("h_scratch", [B, y_len], F32).ap()[:, 0:h_len]
    bn1_dram = nc.dram_tensor("bn1_scratch", [C, 2], F32).ap()
    bn2_dram = nc.dram_tensor("bn2_scratch", [C, 2], F32).ap()
    y_quad, h_quad = (t.rearrange("b (q f) -> b q f", q=P) for t in (y_dram, h_dram))
    y_chan, h_chan = (t.rearrange("b (k p f) -> b p k f", k=J, p=P) for t in (y_dram, h_dram))

    with ExitStack() as ctx:
        def sb(name, shape, dt=F32):
            return ctx.enter_context(nc.sbuf_tensor(name, shape, dt))

        def sem(name):
            return ctx.enter_context(nc.semaphore(name))

        ring_a = sb("ring_a", [P, NS, FB])
        ring_b = sb("ring_b", [P, NS, FB])
        ring_c = sb("ring_c", [P, NS, FB])
        ring_h = sb("ring_h", [P, NS2, FB], F16)
        gT = sb("gT", [P, BANKS, BANK])
        padded = sb("padded", [P, 2, J, NB * PAD * PAD], BF16)
        tuples = sb("tuples", [P, B * J * ST])
        y_tuples = tuples[:, :].rearrange("p (b j s) -> p b j s", j=J, s=ST)
        h_tuples = tuples[:, :].rearrange("p (b j s) -> p b j s", j=J, s=ST)
        gn1 = sb("gn1", [P, B, 2, NB])
        ident = sb("ident", [P, P])
        identb = sb("identb", [P, P], BF16)
        gavg = sb("gavg", [P, P])
        clif = sb("clif", [S, 8, P])
        w0_sb = sb("w0_sb", [S, 8])
        W0T = sb("W0T", [P, P])
        ones = sb("ones", [P, P], BF16)
        bias3 = sb("bias3", [P, BANK], BF16)
        brow = sb("brow", [1, 3, S])
        bpart = sb("bpart", [1, 3, S], BF16)
        cw = sb("cw", [P, J, CG * TAPS])
        cw_cent = sb("cw_cent", [P, J, CG * TAPS])
        cw_sign = sb("cw_sign", [P, J, TAPS, P], BF16)
        conv_wT = sb("conv_wT", [P, J, TAPS, P], BF16)
        wtup = sb("wtup", [P, J, ST])
        wagg = sb("wagg", [P, J, 2])
        wabs = sb("wabs", [P, J])
        wvar = sb("wvar", [P, J])
        wrstd = sb("wrstd", [P, J])
        scale_w = sb("scale_w", [P, J])
        minus_half = sb("minus_half", [P, NB])
        half = sb("half", [P, 1])
        gb1 = sb("gb1", [P, 2, J])
        gb2 = sb("gb2", [P, 2, J])
        slope = sb("slope", [P, 2, J])
        bagg = sb("bagg", [P, J, 2])
        btmp = sb("btmp", [P, 4, J])
        bn1_q = sb("bn1_q", [P, J, 2])
        bn1_c = sb("bn1_c", [P, J, 2])
        bn2_c = sb("bn2_c", [P, J, 2])
        bn2_q = sb("bn2_q", [P, J, 2])
        xs = sb("xs", [P, NB, ST])
        xdev = sb("xdev", [P, 3, NB * 2])
        xve = sb("xve", [P, NB])
        xr = sb("xr", [P, NB])
        xnm = sb("xnm", [P, NB])
        us = sb("us", [P, 2, NB // 2, ST])
        udev = sb("udev", [P, 2, 3, NB])
        uve = sb("uve", [P, 2, NB // 2])
        ur = sb("ur", [P, 2, NB // 2])
        unm = sb("unm", [P, 2, NB // 2])
        gnb = sb("gnb", [P, 2, NB])

        def psum(name, shape):
            return ctx.enter_context(nc.psum_tensor(name, shape, F32))

        psX = psum("psX", [P, BANKS, BANK])
        psT = psum("psT", [P, 2, BANK])
        psS = psum("psS", [P, BANK])
        psW = psum("psW", [P, BANK])
        h_bank = [psX[:, k, :] for k in range(BANKS)] + [psT[:, 0, :], psT[:, 1, :], psS[:, :], psW[:, :]]
        x_mean, x_var = psW[:, 0:8], psW[:, 8:16]
        u_mean = [psS[:, 16 + 8 * u:20 + 8 * u] for u in (UA, UB)]
        u_var = [psS[:, 20 + 8 * u:24 + 8 * u] for u in (UA, UB)]

        const_loaded = sem("const_loaded")
        cleared = sem("cleared")
        prep = sem("prep")
        w0_summed = sem("w0_summed")
        cw_signed = sem("cw_signed")
        cw_turned = sem("cw_turned")
        w_centred = sem("w_centred")
        w_abs_done = sem("w_abs_done")
        w_var_done = sem("w_var_done")
        w_rstd_done = sem("w_rstd_done")
        x_loaded = [sem(f"x_loaded{s}") for s in range(NS)]
        xstat_done = sem("xstat_done")
        xmean_done = sem("xmean_done")
        xdev_step = sem("xdev_step")
        xvar_done = sem("xvar_done")
        xve_done = sem("xve_done")
        xrstd_done = sem("xrstd_done")
        xnm_done = sem("xnm_done")
        g_done = sem("g_done")
        turned = sem("turned")
        gT_done = sem("gT_done")
        x1_done = sem("x1_done")
        ustat_done = sem("ustat_done")
        umean_done = sem("umean_done")
        udev_step = sem("udev_step")
        uvar_done = sem("uvar_done")
        uve_done = sem("uve_done")
        umean_kept = sem("umean_kept")
        urstd_done = sem("urstd_done")
        unm_done = sem("unm_done")
        y_done = sem("y_done")
        ychan_done = sem("ychan_done")
        y_stored = [sem(f"y_stored{s}") for s in range(NS)]
        bn1_step = sem("bn1_step")
        bn1_pow = sem("bn1_pow")
        bn1_ready = sem("bn1_ready")
        bn1_out = sem("bn1_out")
        bn1_in = sem("bn1_in")
        root_done = sem("root_done")
        y2_loaded = [sem(f"y2_loaded{s}") for s in range(NS2)]
        signed = sem("signed")
        conv_done = sem("conv_done")
        h_copied = sem("h_copied")
        h_counted = sem("h_counted")
        h_stored = [sem(f"h_stored{s}") for s in range(NS2)]
        bn2_step = sem("bn2_step")
        bn2_pow = sem("bn2_pow")
        bn2_ready = sem("bn2_ready")
        bn2_out = sem("bn2_out")
        bn2_in = sem("bn2_in")
        y3_loaded = [sem(f"y3_loaded{s}") for s in range(NS)]
        h3_loaded = [sem(f"h3_loaded{s}") for s in range(NS)]
        affine_done = sem("affine_done")
        v_done = sem("v_done")
        relu_done = sem("relu_done")
        gn_copied = sem("gn_copied")
        x1_rebuilt = sem("x1_rebuilt")
        z_done = sem("z_done")
        res_done = sem("res_done")
        out_stored = [sem(f"out_stored{s}") for s in range(NS)]

        def blocks(eng, body, slots):
            loops = (B - HEAD - TAIL[slots]) // slots
            for c in range(HEAD):
                body(0, c)
            with eng.Fori(0, loops) as i:
                for c in range(HEAD, HEAD + slots):
                    body(i, c)
            for c in range(HEAD, HEAD + TAIL[slots]):
                body(loops, c)

        def is_first(i, c, n=1):
            return isinstance(i, int) and i == 0 and c < n

        def is_last(i, c, slots, n=1):
            return isinstance(i, int) and slots * i + c >= B - n

        def row(ap, b):
            if isinstance(b, int):
                return ap[b]
            one = ap[bass.ds(b, 1)]
            return one.rearrange("a p f -> (a p) f") if len(one.shape) == 3 else one.rearrange(
                "a p n f -> (a p) n f")

        def by_sample(tile):
            return tile.rearrange("p (n f) -> p n f", n=NB)

        N_CONST = 12
        BN1_STEPS = J + 1
        block = ctx.enter_context(nc.Block())

        @block.sync
        def _(sp):
            sp.dma_start(by_sample(ring_a[:, 0, :]), xb[0]).then_inc(x_loaded[0], 16)
            for dst, src in ((gavg[:, :], gavg_in), (ident[:, :], ident_in), (clif[:, :, :], clif_in),
                             (brow[:, 0, :], b0.rearrange("(a o) k -> a (o k)", a=1)),
                             (gb1[:, 0, :], g1.rearrange("(q j) -> q j", j=J)),
                             (gb1[:, 1, :], be1.rearrange("(q j) -> q j", j=J)),
                             (slope[:, 0, :], prelu_a.rearrange("(q j) -> q j", j=J)),
                             (cw[:, :, :], conv_w.rearrange("(k p) i a b -> p k (i a b)", p=P)),
                             (gb2[:, 0, :], g2.rearrange("(k p) -> p k", p=P)),
                             (gb2[:, 1, :], be2.rearrange("(k p) -> p k", p=P)),
                             (w0_sb[:, :], w0.rearrange("o i p -> (i p) o"))):
                sp.dma_start(dst, src, allow_slow_non_contiguous=True).then_inc(const_loaded, 16)
            sp.dma_start(slope[:, 1, :], prelu_a.rearrange("(q j) -> q j", j=J)).then_inc(const_loaded, 16)
            sp.dma_start(by_sample(ring_a[:, 1, :]), xb[1]).then_inc(x_loaded[1], 16)

            def store_y(b, s):
                sp.wait_ge(y_done, 4 * b + 4)
                sp.dma_start(row(y_quad, b), ring_c[:, s, :]).then_inc(y_stored[s], 16)

            def pass1(i, c):
                b = NS * i + c
                ahead, before = (c + 2) % NS, (c - 1) % NS
                if not is_last(i, c, NS, 2):
                    if not is_first(i, c):
                        sp.wait_ge(x1_done, 4 * b)
                    sp.dma_start(by_sample(ring_a[:, ahead, :]), row(xb, b + 2)).then_inc(x_loaded[ahead], 16)
                if not is_first(i, c):
                    store_y(b - 1, before)

            blocks(sp, pass1, NS)
            store_y(B - 1, (B - 1) % NS)

            def y2_slot(s):
                return ring_a[:, s, :] if s < NS else ring_b[:, s - NS, :]

            for s in range(NS):
                sp.wait_ge(y_stored[s], 16 * ((B - 1 - s) // NS + 1))
            for s in range(2):
                sp.dma_start(y2_slot(s).rearrange("p (k f) -> p k f", k=J), y_chan[s]).then_inc(y2_loaded[s], 16)
            sp.wait_ge(bn1_ready, 1)
            sp.dma_start(bn1_dram.rearrange("(q j) s -> q (j s)", j=J),
                         bn1_q[:, :, :].rearrange("p j s -> p (j s)")).then_inc(bn1_out, 16)
            sp.wait_ge(bn1_out, 16)
            sp.dma_start(bn1_c[:, :, :], bn1_dram.rearrange("(k p) s -> p k s", p=P),
                         allow_slow_non_contiguous=True).then_inc(bn1_in, 16)

            def h_pairs(s):
                return ring_h[:, s, :].bitcast(F32)

            def store_h(b, s):
                sp.wait_ge(h_copied, 4 * b + 4)
                sp.dma_start(row(h_chan, b), h_pairs(s).rearrange("p (k f) -> p k f", k=J)).then_inc(
                    h_stored[s], 16)

            def pass2(i, c):
                b = NS2 * i + c
                ahead, before = (c + 2) % NS2, (c - 1) % NS2
                if not is_last(i, c, NS2, 2):
                    if not is_first(i, c, 2):
                        sp.wait_ge(signed, 4 * b - 4)
                    sp.dma_start(y2_slot(ahead).rearrange("p (k f) -> p k f", k=J), row(y_chan, b + 2)).then_inc(
                        y2_loaded[ahead], 16)
                if not is_first(i, c):
                    store_h(b - 1, before)

            blocks(sp, pass2, NS2)
            store_h(B - 1, (B - 1) % NS2)

            sp.wait_ge(signed, 4 * B)
            for s in range(2):
                sp.dma_start(ring_a[:, s, :], y_quad[s]).then_inc(y3_loaded[s], 16)
            for s in range(NS2):
                sp.wait_ge(h_stored[s], 16 * ((B - 1 - s) // NS2 + 1))
            sp.wait_ge(h_counted, 4 * B)
            for s in range(2):
                sp.dma_start(h_pairs(s), h_quad[s]).then_inc(h3_loaded[s], 16)
            sp.wait_ge(bn2_ready, 1)
            sp.dma_start(bn2_dram.rearrange("(k p) s -> p k s", p=P), bn2_c[:, :, :],
                         allow_slow_non_contiguous=True).then_inc(bn2_out, 16)
            sp.wait_ge(bn2_out, 16)
            sp.dma_start(bn2_q[:, :, :].rearrange("p j s -> p (j s)"),
                         bn2_dram.rearrange("(q j) s -> q (j s)", j=J)).then_inc(bn2_in, 16)

            def store_result(b, s):
                sp.wait_ge(res_done, b + 1)
                sp.dma_start(row(ob, b), by_sample(ring_c[:, s, :])).then_inc(out_stored[s], 16)

            def pass3(i, c):
                b = NS * i + c
                ahead, before = (c + 2) % NS, (c - 1) % NS
                if not is_last(i, c, NS, 2):
                    if not is_first(i, c):
                        sp.wait_ge(z_done, b)
                    sp.dma_start(h_pairs(ahead), row(h_quad, b + 2)).then_inc(h3_loaded[ahead], 16)
                    sp.dma_start(ring_a[:, ahead, :], row(y_quad, b + 2)).then_inc(y3_loaded[ahead], 16)
                if not is_first(i, c):
                    store_result(b - 1, before)

            blocks(sp, pass3, NS)
            store_result(B - 1, (B - 1) % NS)
            for s in range(NS):
                sp.wait_ge(out_stored[s], 16 * ((B - 1 - s) // NS + 1))

        @block.gpsimd
        def _(pool):
            def rstd_u(u, n):
                pool.wait_ge(uve_done, n + 1)
                pool.tensor_tensor(ur[:, u, :], uve[:, u, :], minus_half[:, 0:NB // 2], ALU.pow).then_inc(urstd_done, 1)

            def rstd_x(b):
                if not (isinstance(b, int) and b == 0):
                    pool.wait_ge(g_done, 4 * b)
                pool.wait_ge(xve_done, b + 1)
                pool.tensor_tensor(xr[:, :], xve[:, :], minus_half[:, :], ALU.pow).then_inc(xrstd_done, 1)

            pool.memset(padded[:, :, :, :].rearrange("p a k f -> p (a k f)"), 0.0).then_inc(cleared, 1)
            pool.wait_ge(w_var_done, 1)
            pool.tensor_tensor(wrstd[:, :], wvar[:, :], minus_half[:, 0:J], ALU.pow).then_inc(w_rstd_done, 1)
            rstd_x(0)

            def pass1(i, c):
                b = NS * i + c
                if not is_first(i, c):
                    rstd_u(UB, 2 * b - 1)
                if not is_last(i, c, NS):
                    rstd_x(b + 1)
                rstd_u(UA, 2 * b)

            blocks(pool, pass1, NS)
            rstd_u(UB, 2 * B - 1)

            pool.wait_ge(bn1_step, BN1_STEPS)
            pool.tensor_tensor(btmp[:, 1, :], btmp[:, 0, :], minus_half[:, 0:J], ALU.pow).then_inc(bn1_pow, 1)
            pool.wait_ge(umean_kept, 2 * B)
            pool.tensor_tensor(gn1[:, :, 1, :], gn1[:, :, 1, :],
                               half[:, 0:1].unsqueeze(2).to_broadcast([P, B, NB]), ALU.pow).then_inc(root_done, 1)
            pool.wait_ge(bn2_step, J + 3)
            pool.tensor_tensor(btmp[:, 3, :], btmp[:, 2, :], minus_half[:, 0:J], ALU.pow).then_inc(bn2_pow, 1)

            def pass3(i, c):
                b = NS * i + c
                s = c % NS
                pool.wait_ge(y3_loaded[s], 16 * (i + c // NS + 1))
                pool.wait_ge(affine_done, b + 1)
                pool.tensor_tensor(ring_b[:, s, :], ring_b[:, s, :], ring_a[:, s, :], ALU.add).then_inc(v_done, 1)

            blocks(pool, pass3, NS)

        @block.scalar
        def _(act):
            act.wait_ge(const_loaded, 16 * N_CONST)
            act.wait_ge(cleared, 2)
            for g in range(P // CG):
                rows = slice(CG * g, CG * g + CG)
                act.activation(cw_sign[rows, :, :, rows],
                               cw[rows, :, :].rearrange("p k (i t) -> p k t i", t=TAPS), ACT.Sign).then_inc(cw_signed, 1)
            act.wait_ge(w_centred, J)
            for k in range(J):
                act.activation(cw_cent[:, k, :], cw_cent[:, k, :], ACT.Abs,
                               accum_out=wabs[:, k:k + 1]).then_inc(w_abs_done, 1)

            def normalise_x(i, c, pairs):
                s = c % NS
                for k in pairs:
                    for n in (PER * k, PER * k + 1):
                        cols = slice(J * S * n, J * S * (n + 1))
                        last = act.activation(ring_b[:, s, cols], ring_a[:, s, cols], ACT.Identity,
                                              bias=xnm[:, n:n + 1], scale=xr[:, n:n + 1])
                    last.then_inc(g_done, 1)

            def copy_turned(b, k):
                act.wait_ge(turned, 4 * b + k + 1)
                act.activation(gT[:, k, :], psT[:, k % 2, :], ACT.Copy).then_inc(gT_done, 1)

            def normalise_x1(i, c, u):
                b = NS * i + c
                s = c % NS
                act.wait_ge(unm_done, 2 * b + u + 1)
                if u == UA and not is_first(i, c, NS):
                    act.wait_ge(y_stored[s], 16 * (i + c // NS))
                    act.wait_ge(ychan_done, b - 2)
                tile = ring_c[:, s, :].rearrange("p (j n s) -> p j n s", j=J, n=NB)
                for k in (2 * u, 2 * u + 1):
                    for h in range(PER):
                        m = PER * (k - 2 * u) + h
                        last = act.activation(
                            tile[:, :, PER * k + h, :],
                            psX[:, k, J * S * h:J * S * (h + 1)].rearrange("p (j s) -> p j s", j=J),
                            ACT.Identity, bias=unm[:, u, m:m + 1], scale=ur[:, u, m:m + 1])
                    last.then_inc(y_done, 1)

            act.wait_ge(xnm_done, 1)
            normalise_x(0, 0, range(4))
            copy_turned(0, 0)

            def pass1(i, c):
                b = NS * i + c
                copy_turned(b, 1)
                if not is_first(i, c):
                    normalise_x1(i, c - 1, UB)
                copy_turned(b, 2)
                if not is_last(i, c, NS):
                    act.wait_ge(xnm_done, b + 2)
                    normalise_x(i, c + 1, (0, 1))
                copy_turned(b, 3)
                if not is_last(i, c, NS):
                    normalise_x(i, c + 1, (2, 3))
                    copy_turned(b + 1, 0)
                normalise_x1(i, c, UA)

            blocks(act, pass1, NS)
            normalise_x1((B - 1) // NS, (B - 1) % NS, UB)

            def y2_slot(s):
                return ring_a[:, s, :] if s < NS else ring_b[:, s - NS, :]

            def take_sign(i, c, k):
                b = NS2 * i + c
                if k == 0:
                    act.wait_ge(y2_loaded[c % NS2], 16 * (i + c // NS2 + 1))
                if not is_first(i, c, 2):
                    act.wait_ge(conv_done, 4 * b - 7 + k)
                frame = padded[:, c % 2, k, :].rearrange("p (n a b) -> p n a b", n=NB, a=PAD)
                act.activation(frame[:, :, 1:1 + SIDE, 1:1 + SIDE],
                               y2_slot(c % NS2).rearrange("p (k n a b) -> p k n a b", k=J, n=NB, a=SIDE)[:, k],
                               ACT.Sign, bias=bn1_c[:, k, 1:2], scale=bn1_c[:, k, 0:1]).then_inc(signed, 1)

            def copy_h(i, c, k):
                b = NS2 * i + c
                act.wait_ge(conv_done, 4 * b + k + 1)
                if k == 0 and not is_first(i, c, NS2):
                    act.wait_ge(h_stored[c % NS2], 16 * (i + c // NS2))
                    act.wait_ge(h_counted, 4 * b - 12)
                act.activation(ring_h[:, c % NS2, BANK * k:BANK * (k + 1)], h_bank[4 * (c % 2) + k],
                               ACT.Copy).then_inc(h_copied, 1)

            act.wait_ge(bn1_in, 16)
            for k in range(J):
                take_sign(0, 0, k)

            def pass2(i, c):
                for k in range(J):
                    if not is_last(i, c, NS2):
                        take_sign(i, c + 1, k)
                    copy_h(i, c, k)

            blocks(act, pass2, NS2)

            def affine_h(i, c):
                b = NS * i + c
                s = c % NS
                act.wait_ge(h3_loaded[s], 16 * (i + c // NS + 1))
                if not is_first(i, c, 3):
                    act.wait_ge(res_done, b - 2)
                for j in range(J):
                    cols = slice(BANK * j, BANK * (j + 1))
                    last = act.activation(ring_b[:, s, cols], ring_h[:, s, cols], ACT.Identity,
                                          bias=bn2_q[:, j, 1:2], scale=bn2_q[:, j, 0:1])
                last.then_inc(affine_done, 1)

            def relu_v(i, c):
                b = NS * i + c
                s = c % NS
                act.wait_ge(v_done, b + 1)
                if not is_first(i, c, NS):
                    act.wait_ge(out_stored[s], 16 * (i + c // NS))
                act.activation(ring_c[:, s, :].rearrange("p (n j s) -> p j n s", n=NB, j=J),
                               ring_b[:, s, :].rearrange("p (j n s) -> p j n s", n=NB, j=J),
                               ACT.Relu).then_inc(relu_done, 1)

            act.wait_ge(bn2_in, 16)
            affine_h(0, 0)

            def pass3(i, c):
                if not is_last(i, c, NS):
                    affine_h(i, c + 1)
                relu_v(i, c)

            blocks(act, pass3, NS)

        @block.vector
        def _(dve):
            steps = [0]

            def step(ins, signal=prep, count=steps):
                count[0] += 1
                ins.then_inc(signal, 1)
                dve.wait_ge(signal, count[0])

            dve.memset(cw_sign[:, :, :, :].rearrange("p k t f -> p (k t f)"), 0.0).then_inc(cleared, 1)
            dve.memset(ones[:, :], 1.0)
            dve.memset(minus_half[:, :], -0.5)
            dve.memset(half[:, :], 0.5)
            dve.memset(bias3[:, :], 0.0)
            step(dve.memset(W0T[:, :], 0.0))
            dve.wait_ge(const_loaded, 16 * N_CONST)

            step(dve.tensor_copy(identb[:, :], ident[:, :]))
            for n in range(3):
                step(dve.tensor_copy(bpart[:, n, :], brow[:, n, :]))
                if n < 2:
                    step(dve.tensor_tensor(brow[:, n + 1, :], brow[:, n, :], bpart[:, n, :], ALU.subtract))
                step(dve.tensor_copy(bias3[32 * n:32 * n + 1, :].rearrange("p (r f) -> p r f", f=S),
                                     bpart[:, n:n + 1, :].to_broadcast([1, BANK // S, S])))
            taken = CG * TAPS
            for k in range(J):
                step(dve.bn_stats(wtup[:, k, :], cw[:, k, :]))
                step(dve.bn_aggr(wagg[:, k, :], wtup[:, k, :]))
                dve.tensor_scalar(cw_cent[:, k, :], cw[:, k, :], wagg[:, k, 0:1], None,
                                  ALU.subtract).then_inc(w_centred, 1)
            dve.tensor_scalar(wvar[:, :], wagg[:, :, 1], taken / (taken - 1), None, ALU.mult).then_inc(w_var_done, 1)
            dve.wait_ge(w_rstd_done, 1)
            dve.wait_ge(w_abs_done, J)
            step(dve.tensor_scalar(scale_w[:, :], wabs[:, :], 1.0 / taken, None, ALU.mult))
            step(dve.tensor_tensor(scale_w[:, :], scale_w[:, :], wrstd[:, :], ALU.mult))
            step(dve.tensor_scalar(slope[:, 1, :], slope[:, 1, :], -1.0, 1.0, ALU.mult, ALU.add))
            dve.wait_ge(w0_summed, 1)
            for d in range(2):
                rows = slice(S * d, S * d + S)
                step(dve.tensor_copy(W0T[rows, rows].rearrange("p (o k) -> p k o", k=8),
                                     psW[rows, 0:S].rearrange("p (k o) -> p k o", k=8)))
            for k in range(J):
                dve.wait_ge(cw_turned, k + 1)
                step(dve.tensor_copy(conv_wT[:, k, :, :].rearrange("p t f -> p (t f)"),
                                     psX[:, 0:2, :].rearrange("p a f -> p (a f)").bitcast(BF16)[:, 0:TAPS * P]))

            def stat_x(i, c, samples):
                s = c % NS
                for n in samples:
                    last = dve.bn_stats(xs[:, n, :], ring_a[:, s, J * S * n:J * S * (n + 1)])
                return last

            def halves(tup, n, at):
                return tup.rearrange("p n (h s) -> p n h s", s=3)[:, :, :, at]

            def deviations(tup, mean, dev, n, signal, before):
                d = [dev[:, m, :].rearrange("p (n h) -> p n h", h=2) for m in range(3)]
                dve.tensor_tensor(d[0], halves(tup, n, 1), mean.unsqueeze(2).to_broadcast([P, n, 2]),
                                  ALU.subtract).then_inc(signal, 1)
                dve.wait_ge(signal, before + 1)
                dve.tensor_tensor(d[1], d[0], d[0], ALU.mult).then_inc(signal, 1)
                dve.wait_ge(signal, before + 2)
                dve.scalar_tensor_tensor(out=d[2], in0=halves(tup, n, 2), scalar=2.0 / (J * S), in1=d[1],
                                         op0=ALU.mult, op1=ALU.add).then_inc(signal, 1)

            def x_deviations(b):
                dve.wait_ge(xmean_done, b + 1)
                deviations(xs[:, :, :], x_mean, xdev, NB, xdev_step, 3 * b)

            def x_variance(b):
                dve.wait_ge(xvar_done, b + 1)
                dve.tensor_scalar(xve[:, :], x_var, EPS, None, ALU.add).then_inc(xve_done, 1)

            def x_addend(b):
                dve.wait_ge(xrstd_done, b + 1)
                dve.scalar_tensor_tensor(out=xnm[:, :], in0=x_mean, scalar=-1.0, in1=xr[:, :],
                                         op0=ALU.mult, op1=ALU.mult).then_inc(xnm_done, 1)

            def stat_x1(b, k):
                dve.wait_ge(x1_done, 4 * b + k + 1)
                for h in range(PER):
                    last = dve.bn_stats(us[:, k // 2, PER * (k % 2) + h, :], psX[:, k, J * S * h:J * S * (h + 1)])
                if k % 2:
                    last.then_inc(ustat_done, 1)

            def u_deviations(b, u):
                dve.wait_ge(umean_done, 2 * b + u + 1)
                deviations(us[:, u, :, :], u_mean[u], udev[:, u], NB // 2, udev_step, 6 * b + 3 * u)

            def u_variance(b, u):
                half_of = slice(NB // 2 * u, NB // 2 * (u + 1))
                dve.wait_ge(uvar_done, 2 * b + u + 1)
                dve.tensor_scalar(uve[:, u, :], u_var[u], EPS, None, ALU.add).then_inc(uve_done, 1)
                at = b if isinstance(b, int) else None
                kept = gn1[:, at, :, half_of] if at is not None else gn1[:, bass.ds(b, 1), :, half_of].rearrange(
                    "p a m n -> p (a m) n")
                both = psS[:, 16 + 8 * u:24 + 8 * u].rearrange("p (m n) -> p m n", m=2)
                dve.tensor_scalar(kept[:, 0, :], both[:, 0, :], 0.0, None, ALU.add)
                dve.tensor_scalar(kept[:, 1, :], both[:, 1, :], EPS, None, ALU.add).then_inc(umean_kept, 1)

            def u_addend(b, u):
                dve.wait_ge(urstd_done, 2 * b + u + 1)
                dve.scalar_tensor_tensor(out=unm[:, u, :], in0=u_mean[u], scalar=-1.0, in1=ur[:, u, :],
                                         op0=ALU.mult, op1=ALU.mult).then_inc(unm_done, 1)

            def count_y(i, c, j):
                b = NS * i + c
                if j == 0:
                    dve.wait_ge(y_done, 4 * b + 4)
                to = y_tuples[:, b, j, :] if isinstance(b, int) else y_tuples[:, bass.ds(b, 1), j, :].rearrange(
                    "p a s -> p (a s)")
                last = dve.bn_stats(to, ring_c[:, c % NS, BANK * j:BANK * (j + 1)])
                if j == J - 1:
                    last.then_inc(ychan_done, 1)

            dve.wait_ge(x_loaded[0], 16)
            stat_x(0, 0, range(NB)).then_inc(xstat_done, 1)
            x_deviations(0)
            x_variance(0)
            x_addend(0)

            def pass1(i, c):
                b = NS * i + c
                before = not is_first(i, c)
                after = not is_last(i, c, NS)
                if before:
                    stat_x1(b - 1, 3)
                if after:
                    dve.wait_ge(x_loaded[(c + 1) % NS], 16 * (i + (c + 1) // NS + 1))
                    stat_x(i, c + 1, range(0, 4))
                if before:
                    u_deviations(b - 1, UB)
                stat_x1(b, 0)
                if after:
                    stat_x(i, c + 1, range(4, 6))
                if before:
                    u_variance(b - 1, UB)
                if after:
                    stat_x(i, c + 1, range(6, 8)).then_inc(xstat_done, 1)
                if before:
                    u_addend(b - 1, UB)
                if after:
                    x_deviations(b + 1)
                stat_x1(b, 1)
                if after:
                    x_variance(b + 1)
                if before:
                    count_y(i, c - 1, 0)
                    count_y(i, c - 1, 1)
                if after:
                    x_addend(b + 1)
                u_deviations(b, UA)
                if before:
                    count_y(i, c - 1, 2)
                u_variance(b, UA)
                stat_x1(b, 2)
                u_addend(b, UA)
                if before:
                    count_y(i, c - 1, 3)

            blocks(dve, pass1, NS)
            stat_x1(B - 1, 3)
            u_deviations(B - 1, UB)
            u_variance(B - 1, UB)
            u_addend(B - 1, UB)
            for j in range(J):
                count_y((B - 1) // NS, (B - 1) % NS, j)

            done = [0]
            dve.wait_ge(ychan_done, B)
            for j in range(J):
                step(dve.bn_aggr(bagg[:, j, :], y_tuples[:, :, j, :]), bn1_step, done)
            step(dve.tensor_scalar(btmp[:, 0, :], bagg[:, :, 1], EPS, None, ALU.add), bn1_step, done)
            dve.wait_ge(bn1_pow, 1)
            step(dve.tensor_tensor(bn1_q[:, :, 0], gb1[:, 0, :], btmp[:, 1, :], ALU.mult), bn1_step, done)
            step(dve.tensor_tensor(btmp[:, 2, :], bagg[:, :, 0], bn1_q[:, :, 0], ALU.mult), bn1_step, done)
            dve.tensor_tensor(bn1_q[:, :, 1], gb1[:, 1, :], btmp[:, 2, :], ALU.subtract).then_inc(bn1_ready, 1)

            def pass2(i, c):
                b = NS2 * i + c
                for k in range(J):
                    dve.wait_ge(h_copied, 4 * b + k + 1)
                    to = h_tuples[:, b, k, :] if isinstance(b, int) else h_tuples[:, bass.ds(b, 1), k, :].rearrange(
                        "p a s -> p (a s)")
                    dve.bn_stats(to, ring_h[:, c % NS2, BANK * k:BANK * (k + 1)]).then_inc(h_counted, 1)

            blocks(dve, pass2, NS2)

            done = [0]
            dve.wait_ge(h_counted, 4 * B)
            for k in range(J):
                step(dve.bn_aggr(bagg[:, k, :], h_tuples[:, :, k, :]), bn2_step, done)
            step(dve.tensor_tensor(btmp[:, 0, :], bagg[:, :, 1], scale_w[:, :], ALU.mult), bn2_step, done)
            step(dve.tensor_tensor(btmp[:, 1, :], btmp[:, 0, :], scale_w[:, :], ALU.mult), bn2_step, done)
            step(dve.tensor_scalar(btmp[:, 2, :], btmp[:, 1, :], EPS, None, ALU.add), bn2_step, done)
            dve.wait_ge(bn2_pow, 1)
            step(dve.tensor_tensor(btmp[:, 0, :], gb2[:, 0, :], scale_w[:, :], ALU.mult), bn2_step, done)
            step(dve.tensor_tensor(bn2_c[:, :, 0], btmp[:, 0, :], btmp[:, 3, :], ALU.mult), bn2_step, done)
            step(dve.tensor_tensor(btmp[:, 1, :], bagg[:, :, 0], bn2_c[:, :, 0], ALU.mult), bn2_step, done)
            dve.tensor_tensor(bn2_c[:, :, 1], gb2[:, 1, :], btmp[:, 1, :], ALU.subtract).then_inc(bn2_ready, 1)
            dve.wait_ge(root_done, 1)

            def pass3(i, c):
                b = NS * i + c
                s = c % NS
                stats = gn1[:, b, :, :] if isinstance(b, int) else gn1[:, bass.ds(b, 1), :, :].rearrange(
                    "p a m n -> p (a m) n")
                if not is_first(i, c):
                    dve.wait_ge(x1_rebuilt, b)
                dve.tensor_copy(gnb[:, :, :], stats).then_inc(gn_copied, 1)
                dve.wait_ge(gn_copied, b + 1)
                dve.wait_ge(v_done, b + 1)
                y = ring_a[:, s, :].rearrange("p (j n s) -> p j n s", j=J, n=NB)
                for n in range(NB):
                    last = dve.tensor_scalar(y[:, :, n, :], y[:, :, n, :], gnb[:, 1, n:n + 1], gnb[:, 0, n:n + 1],
                                             ALU.mult, ALU.add)
                last.then_inc(x1_rebuilt, 1)
                dve.wait_ge(x1_rebuilt, b + 1)
                dve.wait_ge(relu_done, b + 1)
                for j in range(J):
                    cols = slice(BANK * j, BANK * (j + 1))
                    last = dve.scalar_tensor_tensor(out=ring_b[:, s, cols], in0=ring_b[:, s, cols],
                                                    scalar=slope[:, 0, j:j + 1], in1=ring_a[:, s, cols],
                                                    op0=ALU.mult, op1=ALU.add)
                last.then_inc(z_done, 1)
                dve.wait_ge(z_done, b + 1)
                res = ring_c[:, s, :].rearrange("p (n j s) -> p j n s", n=NB, j=J)
                for j in range(J):
                    last = dve.scalar_tensor_tensor(
                        out=res[:, j], in0=res[:, j], scalar=slope[:, 1, j:j + 1],
                        in1=ring_b[:, s, BANK * j:BANK * (j + 1)].rearrange("p (n s) -> p n s", n=NB),
                        op0=ALU.mult, op1=ALU.add)
                last.then_inc(res_done, 1)

            blocks(dve, pass3, NS)

        @block.tensor
        def _(pe):
            def turn(i, c, k):
                b = NS * i + c
                s = c % NS
                pe.wait_ge(g_done, 4 * b + k + 1)
                if not (is_first(i, c) and k < 2):
                    pe.wait_ge(gT_done, 4 * b + k - 1)
                for m in range(4):
                    last = pe.transpose(psT[:, k % 2, P * m:P * (m + 1)],
                                        ring_b[:, s, BANK * k + P * m:BANK * k + P * (m + 1)], ident[:, :])
                last.then_inc(turned, 1)

            def product(k, m):
                return pe.matmul(psX[:, k, P * m:P * (m + 1)], gT[:, k, P * m:P * (m + 1)], W0T[:, :],
                                 start=False, stop=(m == 3))

            def begin_bank(i, c, k):
                b = NS * i + c
                if not is_first(i, c):
                    pe.wait_ge(y_done, 4 * b - 3 + k)
                pe.matmul(psX[:, k, :], ident[:, :], ring_a[:, c % NS, BANK * k:BANK * (k + 1)],
                          start=True, stop=False)
                pe.matmul(psX[:, k, :], ones[:, :], bias3[:, :], start=False, stop=False)
                pe.wait_ge(gT_done, 4 * b + k + 1)
                product(k, 0)
                product(k, 1)

            def end_bank(k):
                product(k, 2)
                product(k, 3).then_inc(x1_done, 1)

            def mean_of(dst, tup, signal):
                pe.matmul(dst, gavg[:, :], tup[:, :, 1], start=True, stop=False)
                pe.matmul(dst, gavg[:, :], tup[:, :, 4], start=False, stop=True).then_inc(signal, 1)

            def var_of(dst, dev, signal):
                d = dev.rearrange("p (n h) -> p n h", h=2)
                pe.matmul(dst, gavg[:, :], d[:, :, 0], start=True, stop=False)
                pe.matmul(dst, gavg[:, :], d[:, :, 1], start=False, stop=True).then_inc(signal, 1)

            def x_mean_of(b):
                pe.wait_ge(xstat_done, b + 1)
                mean_of(x_mean, xs, xmean_done)

            def x_var_of(b):
                pe.wait_ge(xdev_step, 3 * b + 3)
                var_of(x_var, xdev[:, 2, :], xvar_done)

            def u_mean_of(b, u):
                pe.wait_ge(ustat_done, 2 * b + u + 1)
                if not (isinstance(b, int) and b == 0 and u == UA):
                    pe.wait_ge(unm_done, 2 * b + u)
                mean_of(u_mean[u], us[:, u], umean_done)

            def u_var_of(b, u):
                pe.wait_ge(udev_step, 6 * b + 3 * u + 3)
                var_of(u_var[u], udev[:, u, 2, :], uvar_done)

            pe.wait_ge(const_loaded, 16 * N_CONST)
            for k in range(8):
                last = pe.matmul(psW[:, 8 * k:8 * k + 8], clif[:, k, :], w0_sb[:, :], start=True, stop=True)
            last.then_inc(w0_summed, 1)
            pe.wait_ge(cw_signed, P // CG)
            turned_w = psX[:, 0:2, :].rearrange("p a f -> p (a f)").bitcast(BF16)
            first_copy = 23
            for k in range(J):
                pe.wait_ge(prep, first_copy + k)
                for t in range(TAPS):
                    last = pe.transpose(turned_w[:, P * t:P * (t + 1)], cw_sign[:, k, t, :], identb[:, :])
                last.then_inc(cw_turned, 1)

            x_mean_of(0)
            x_var_of(0)
            turn(0, 0, 0)
            pe.wait_ge(prep, first_copy + J)

            def pass1(i, c):
                b = NS * i + c
                before = not is_first(i, c)
                after = not is_last(i, c, NS)
                turn(i, c, 1)
                begin_bank(i, c, 0)
                if before:
                    u_mean_of(b - 1, UB)
                end_bank(0)
                if before:
                    u_var_of(b - 1, UB)
                turn(i, c, 2)
                begin_bank(i, c, 1)
                if after:
                    x_mean_of(b + 1)
                end_bank(1)
                if after:
                    x_var_of(b + 1)
                turn(i, c, 3)
                begin_bank(i, c, 2)
                u_mean_of(b, UA)
                end_bank(2)
                u_var_of(b, UA)
                if after:
                    turn(i, c + 1, 0)
                begin_bank(i, c, 3)
                end_bank(3)

            blocks(pe, pass1, NS)
            u_mean_of(B - 1, UB)
            u_var_of(B - 1, UB)

            pe.wait_ge(cleared, 2)
            pe.wait_ge(y_done, 4 * B)
            pe.wait_ge(unm_done, 2 * B)

            def pass2(i, c):
                b = NS2 * i + c
                for k in range(J):
                    pe.wait_ge(signed, 4 * b + k + 1)
                    if not is_first(i, c, 2):
                        pe.wait_ge(h_copied, 4 * b - 7 + k)
                    frame = padded[:, c % 2, k, :].rearrange("p (n a b) -> p n a b", n=NB, a=PAD)
                    for t in range(TAPS):
                        dy, dx = t // 3, t % 3
                        last = pe.matmul(h_bank[4 * (c % 2) + k], conv_wT[:, k, t, :],
                                         frame[:, :, dy:dy + SIDE, dx:dx + SIDE],
                                         start=(t == 0), stop=(t == TAPS - 1))
                    last.then_inc(conv_done, 1)

            blocks(pe, pass2, NS2)


_NAMES = ["x", "L0_conv_weight", "L0_conv_bias", "L1_conv_conv_w", "L1_conv_bn1_gamma", "L1_conv_bn1_beta",
          "L1_conv_bn2_gamma", "L1_conv_bn2_beta", "L1_conv_prelu_a"]


def constants():
    group = np.kron(np.eye(P // 4), np.full((4, 4), 1 / 8)).astype(np.float32)
    sel = np.einsum("kpq,ij->ipkjq", clifford_terms(), np.eye(8, dtype=np.float32)).reshape(S, 8, S)
    return {"identity": np.eye(P, dtype=np.float32), "group_average": group,
            "algebra": np.ascontiguousarray(np.concatenate([sel, sel], axis=2))}


def kernel(**inputs):
    import concourse.bacc as bacc
    from concourse.bass_utils import run_bass_kernel_spmd

    nc = bacc.Bacc("TRN2", target_bir_lowering=False, num_devices=1)
    arrays = {f"in_{n}": np.ascontiguousarray(inputs[n]) for n in _NAMES}
    arrays.update(constants())
    args = [nc.dram_tensor(n, a.shape, mybir.dt.from_np(a.dtype), kind="ExternalInput").ap()
            for n, a in arrays.items()]
    out = nc.dram_tensor("out", inputs["x"].shape, F32, kind="ExternalOutput").ap()
    two_layer_kernel(nc, *args, out)
    r = run_bass_kernel_spmd(nc, [arrays], core_ids=[0])
    return r.results[0]["out"]
```

```python
from contextlib import ExitStack

import numpy as np

import concourse.bass as bass
from concourse import mybir

ALU = mybir.AluOpType
ACT = mybir.ActivationFunctionType
F32 = mybir.dt.float32
F16 = mybir.dt.float16
BF16 = mybir.dt.bfloat16

P = 128
C = 512
S = 64
SIDE = 8
J = C // P
NB = 8
FB = NB * J * S
BANK = 512
BANKS = FB // BANK
PER = NB // BANKS
RING = 6
NS = 3
NS2 = 4
EPS = 1e-5
ST = 6
TAPS = 9
PAD = SIDE + 2
CG = 32
UA, UB = 0, 1


SIGNS = ['++++----', '+++--+--', '+-+++--+', '+--++-+-', '+-+-++-+', '++---+++', '+++-+-+-', '++-++-++']


def clifford_terms():
    bits = [0, 1, 2, 4, 3, 5, 6, 7]
    table = np.zeros((8, 8, 8), np.float32)
    for k in range(8):
        for q in range(8):
            table[k, bits.index(bits[k] ^ bits[q]), q] = 1.0 if SIGNS[k][q] == "+" else -1.0
    return table


def two_layer_kernel(nc, x, w0, b0, conv_w, g1, be1, g2, be2, prelu_a, ident_in, gavg_in, clif_in, out):
    N = x.shape[0]
    B = N // NB
    HEAD, TAIL = 4, {NS: 3, NS2: 4}
    assert B * NB == N and all(B > HEAD + t and (B - HEAD - t) % slots == 0 for slots, t in TAIL.items())

    xb = x.rearrange("(b n) (q j) h w -> b q n (j h w)", n=NB, j=J)
    ob = out.rearrange("(b n) (q j) h w -> b q n (j h w)", n=NB, j=J)
    y_len, h_len = C * NB * S, C * NB * S // 2
    y_dram = nc.dram_tensor("y_scratch", [B, y_len], F32).ap()
    h_dram = nc.dram_tensor("h_scratch", [B, y_len], F32).ap()[:, 0:h_len]
    bn1_dram = nc.dram_tensor("bn1_scratch", [C, 2], F32).ap()
    bn2_dram = nc.dram_tensor("bn2_scratch", [C, 2], F32).ap()
    y_quad, h_quad = (t.rearrange("b (q f) -> b q f", q=P) for t in (y_dram, h_dram))
    y_chan, h_chan = (t.rearrange("b (k p f) -> b p k f", k=J, p=P) for t in (y_dram, h_dram))

    with ExitStack() as ctx:
        def sb(name, shape, dt=F32):
            return ctx.enter_context(nc.sbuf_tensor(name, shape, dt))

        def sem(name):
            return ctx.enter_context(nc.semaphore(name))

        ring_a = sb("ring_a", [P, NS, FB])
        ring_b = sb("ring_b", [P, NS, FB])
        ring_c = sb("ring_c", [P, NS, FB])
        ring_h = sb("ring_h", [P, NS2, FB], F16)
        gT = sb("gT", [P, BANKS, BANK])
        padded = sb("padded", [P, 2, J, NB * PAD * PAD], BF16)
        tuples = sb("tuples", [P, B * J * ST])
        y_tuples = tuples[:, :].rearrange("p (b j s) -> p b j s", j=J, s=ST)
        h_tuples = tuples[:, :].rearrange("p (b j s) -> p b j s", j=J, s=ST)
        gn1 = sb("gn1", [P, B, 2, NB])
        ident = sb("ident", [P, P])
        identb = sb("identb", [P, P], BF16)
        gavg = sb("gavg", [P, P])
        clif = sb("clif", [S, 8, P])
        w0_sb = sb("w0_sb", [S, 8])
        W0T = sb("W0T", [P, P])
        ones = sb("ones", [P, P], BF16)
        bias3 = sb("bias3", [P, BANK], BF16)
        brow = sb("brow", [1, 3, S])
        bpart = sb("bpart", [1, 3, S], BF16)
        cw = sb("cw", [P, J, CG * TAPS])
        cw_cent = sb("cw_cent", [P, J, CG * TAPS])
        cw_sign = sb("cw_sign", [P, J, TAPS, P], BF16)
        conv_wT = sb("conv_wT", [P, J, TAPS, P], BF16)
        wtup = sb("wtup", [P, J, ST])
        wagg = sb("wagg", [P, J, 2])
        wabs = sb("wabs", [P, J])
        wvar = sb("wvar", [P, J])
        wrstd = sb("wrstd", [P, J])
        scale_w = sb("scale_w", [P, J])
        minus_half = sb("minus_half", [P, NB])
        half = sb("half", [P, 1])
        gb1 = sb("gb1", [P, 2, J])
        gb2 = sb("gb2", [P, 2, J])
        slope = sb("slope", [P, 2, J])
        bagg = sb("bagg", [P, J, 2])
        btmp = sb("btmp", [P, 4, J])
        bn1_q = sb("bn1_q", [P, J, 2])
        bn1_c = sb("bn1_c", [P, J, 2])
        bn2_c = sb("bn2_c", [P, J, 2])
        bn2_q = sb("bn2_q", [P, J, 2])
        xs = sb("xs", [P, NB, ST])
        xsum = sb("xsum", [P, NB])
        xdev = sb("xdev", [P, 3, NB * 2])
        xdevs = sb("xdevs", [P, NB])
        xve = sb("xve", [P, NB])
        xr = sb("xr", [P, NB])
        xnm = sb("xnm", [P, NB])
        us = sb("us", [P, 2, NB // 2, ST])
        usum = sb("usum", [P, 2, NB // 2])
        udev = sb("udev", [P, 2, 3, NB])
        udevs = sb("udevs", [P, 2, NB // 2])
        mean_eps = sb("mean_eps", [P, 2, NB // 2])
        ur = sb("ur", [P, 2, NB // 2])
        unm = sb("unm", [P, 2, NB // 2])
        gnb = sb("gnb", [P, 2, NB])

        def psum(name, shape):
            return ctx.enter_context(nc.psum_tensor(name, shape, F32))

        psX = psum("psX", [P, RING, BANK])
        psS = psum("psS", [P, BANK])
        psW = psum("psW", [P, BANK])
        h_bank = [psX[:, k, :] for k in range(RING)] + [psS[:, :], psW[:, :]]
        x_mean, x_var = psW[:, 0:8], psW[:, 8:16]
        u_mean = [psS[:, 16 + 8 * u:20 + 8 * u] for u in (UA, UB)]
        u_var = [psS[:, 20 + 8 * u:24 + 8 * u] for u in (UA, UB)]

        const_loaded = sem("const_loaded")
        cleared = sem("cleared")
        prep = sem("prep")
        w0_summed = sem("w0_summed")
        cw_signed = sem("cw_signed")
        cw_turned = sem("cw_turned")
        w_centred = sem("w_centred")
        w_abs_done = sem("w_abs_done")
        w_var_done = sem("w_var_done")
        w_rstd_done = sem("w_rstd_done")
        x_loaded = [sem(f"x_loaded{s}") for s in range(NS)]
        xbn_done = sem("xbn_done")
        xsum_done = sem("xsum_done")
        xmean_done = sem("xmean_done")
        xdev_step = sem("xdev_step")
        xdev_done = sem("xdev_done")
        xvar_done = sem("xvar_done")
        xve_done = sem("xve_done")
        xrstd_done = sem("xrstd_done")
        xnm_done = sem("xnm_done")
        g_done = sem("g_done")
        turned = sem("turned")
        gT_done = sem("gT_done")
        x1_done = sem("x1_done")
        ubn_done = sem("ubn_done")
        usum_done = sem("usum_done")
        umean_done = sem("umean_done")
        udev_step = sem("udev_step")
        udev_done = sem("udev_done")
        uvar_done = sem("uvar_done")
        ukept = sem("ukept")
        urstd_done = sem("urstd_done")
        unm_done = sem("unm_done")
        y_done = sem("y_done")
        ychan_done = sem("ychan_done")
        y_stored = [sem(f"y_stored{s}") for s in range(NS)]
        bn1_step = sem("bn1_step")
        bn1_pow = sem("bn1_pow")
        bn1_ready = sem("bn1_ready")
        bn1_out = sem("bn1_out")
        bn1_in = sem("bn1_in")
        root_done = sem("root_done")
        y2_loaded = [sem(f"y2_loaded{s}") for s in range(NS2)]
        signed = sem("signed")
        conv_done = sem("conv_done")
        h_copied = sem("h_copied")
        h_counted = sem("h_counted")
        h_stored = [sem(f"h_stored{s}") for s in range(NS2)]
        bn2_step = sem("bn2_step")
        bn2_pow = sem("bn2_pow")
        bn2_ready = sem("bn2_ready")
        bn2_out = sem("bn2_out")
        bn2_in = sem("bn2_in")
        y3_loaded = [sem(f"y3_loaded{s}") for s in range(NS)]
        h3_loaded = [sem(f"h3_loaded{s}") for s in range(NS)]
        affine_done = sem("affine_done")
        v_done = sem("v_done")
        relu_done = sem("relu_done")
        gn_copied = sem("gn_copied")
        x1_rebuilt = sem("x1_rebuilt")
        z_done = sem("z_done")
        res_done = sem("res_done")
        out_stored = [sem(f"out_stored{s}") for s in range(NS)]

        def blocks(eng, body, slots):
            loops = (B - HEAD - TAIL[slots]) // slots
            for c in range(HEAD):
                body(0, c)
            with eng.Fori(0, loops) as i:
                for c in range(HEAD, HEAD + slots):
                    body(i, c)
            for c in range(HEAD, HEAD + TAIL[slots]):
                body(loops, c)

        def is_first(i, c, n=1):
            return isinstance(i, int) and i == 0 and c < n

        def is_last(i, c, slots, n=1):
            return isinstance(i, int) and slots * i + c >= B - n

        def row(ap, b):
            if isinstance(b, int):
                return ap[b]
            one = ap[bass.ds(b, 1)]
            return one.rearrange("a p f -> (a p) f") if len(one.shape) == 3 else one.rearrange(
                "a p n f -> (a p) n f")

        def bank_of(c, k):
            return psX[:, (BANKS * c + k) % RING, :]

        def kept(b, u):
            four = slice(NB // 2 * u, NB // 2 * (u + 1))
            return gn1[:, b, :, four] if isinstance(b, int) else gn1[:, bass.ds(b, 1), :, four].rearrange(
                "p a m n -> p (a m) n")

        def by_sample(tile):
            return tile.rearrange("p (n f) -> p n f", n=NB)

        N_CONST = 12
        BN1_STEPS = J + 1
        block = ctx.enter_context(nc.Block())

        @block.sync
        def _(sp):
            sp.dma_start(by_sample(ring_a[:, 0, :]), xb[0]).then_inc(x_loaded[0], 16)
            for dst, src in ((gavg[:, :], gavg_in), (ident[:, :], ident_in), (clif[:, :, :], clif_in),
                             (brow[:, 0, :], b0.rearrange("(a o) k -> a (o k)", a=1)),
                             (gb1[:, 0, :], g1.rearrange("(q j) -> q j", j=J)),
                             (gb1[:, 1, :], be1.rearrange("(q j) -> q j", j=J)),
                             (slope[:, 0, :], prelu_a.rearrange("(q j) -> q j", j=J)),
                             (cw[:, :, :], conv_w.rearrange("(k p) i a b -> p k (i a b)", p=P)),
                             (gb2[:, 0, :], g2.rearrange("(k p) -> p k", p=P)),
                             (gb2[:, 1, :], be2.rearrange("(k p) -> p k", p=P)),
                             (w0_sb[:, :], w0.rearrange("o i p -> (i p) o"))):
                sp.dma_start(dst, src, allow_slow_non_contiguous=True).then_inc(const_loaded, 16)
            sp.dma_start(slope[:, 1, :], prelu_a.rearrange("(q j) -> q j", j=J)).then_inc(const_loaded, 16)
            sp.dma_start(by_sample(ring_a[:, 1, :]), xb[1]).then_inc(x_loaded[1], 16)

            def store_y(b, s):
                sp.wait_ge(y_done, 4 * b + 4)
                sp.dma_start(row(y_quad, b), ring_c[:, s, :]).then_inc(y_stored[s], 16)

            def pass1(i, c):
                b = NS * i + c
                ahead, before = (c + 2) % NS, (c - 1) % NS
                if not is_last(i, c, NS, 2):
                    if not is_first(i, c):
                        sp.wait_ge(x1_done, 4 * b)
                    sp.dma_start(by_sample(ring_a[:, ahead, :]), row(xb, b + 2)).then_inc(x_loaded[ahead], 16)
                if not is_first(i, c):
                    store_y(b - 1, before)

            blocks(sp, pass1, NS)
            store_y(B - 1, (B - 1) % NS)

            def y2_slot(s):
                return ring_a[:, s, :] if s < NS else ring_b[:, s - NS, :]

            for s in range(NS):
                sp.wait_ge(y_stored[s], 16 * ((B - 1 - s) // NS + 1))
            for s in range(2):
                sp.dma_start(y2_slot(s).rearrange("p (k f) -> p k f", k=J), y_chan[s]).then_inc(y2_loaded[s], 16)
            sp.wait_ge(bn1_ready, 1)
            sp.dma_start(bn1_dram.rearrange("(q j) s -> q (j s)", j=J),
                         bn1_q[:, :, :].rearrange("p j s -> p (j s)")).then_inc(bn1_out, 16)
            sp.wait_ge(bn1_out, 16)
            sp.dma_start(bn1_c[:, :, :], bn1_dram.rearrange("(k p) s -> p k s", p=P),
                         allow_slow_non_contiguous=True).then_inc(bn1_in, 16)

            def h_pairs(s):
                return ring_h[:, s, :].bitcast(F32)

            def store_h(b, s):
                sp.wait_ge(h_copied, 4 * b + 4)
                sp.dma_start(row(h_chan, b), h_pairs(s).rearrange("p (k f) -> p k f", k=J)).then_inc(
                    h_stored[s], 16)

            def pass2(i, c):
                b = NS2 * i + c
                ahead, before = (c + 2) % NS2, (c - 1) % NS2
                if not is_last(i, c, NS2, 2):
                    if not is_first(i, c, 2):
                        sp.wait_ge(signed, 4 * b - 4)
                    sp.dma_start(y2_slot(ahead).rearrange("p (k f) -> p k f", k=J), row(y_chan, b + 2)).then_inc(
                        y2_loaded[ahead], 16)
                if not is_first(i, c):
                    store_h(b - 1, before)

            blocks(sp, pass2, NS2)
            store_h(B - 1, (B - 1) % NS2)

            sp.wait_ge(signed, 4 * B)
            for s in range(2):
                sp.dma_start(ring_a[:, s, :], y_quad[s]).then_inc(y3_loaded[s], 16)
            for s in range(NS2):
                sp.wait_ge(h_stored[s], 16 * ((B - 1 - s) // NS2 + 1))
            sp.wait_ge(h_counted, 4 * B)
            for s in range(2):
                sp.dma_start(h_pairs(s), h_quad[s]).then_inc(h3_loaded[s], 16)
            sp.wait_ge(bn2_ready, 1)
            sp.dma_start(bn2_dram.rearrange("(k p) s -> p k s", p=P), bn2_c[:, :, :],
                         allow_slow_non_contiguous=True).then_inc(bn2_out, 16)
            sp.wait_ge(bn2_out, 16)
            sp.dma_start(bn2_q[:, :, :].rearrange("p j s -> p (j s)"),
                         bn2_dram.rearrange("(q j) s -> q (j s)", j=J)).then_inc(bn2_in, 16)

            def store_result(b, s):
                sp.wait_ge(res_done, b + 1)
                sp.dma_start(row(ob, b), by_sample(ring_c[:, s, :])).then_inc(out_stored[s], 16)

            def pass3(i, c):
                b = NS * i + c
                ahead, before = (c + 2) % NS, (c - 1) % NS
                if not is_last(i, c, NS, 2):
                    if not is_first(i, c):
                        sp.wait_ge(z_done, b)
                    sp.dma_start(h_pairs(ahead), row(h_quad, b + 2)).then_inc(h3_loaded[ahead], 16)
                    sp.dma_start(ring_a[:, ahead, :], row(y_quad, b + 2)).then_inc(y3_loaded[ahead], 16)
                if not is_first(i, c):
                    store_result(b - 1, before)

            blocks(sp, pass3, NS)
            store_result(B - 1, (B - 1) % NS)
            for s in range(NS):
                sp.wait_ge(out_stored[s], 16 * ((B - 1 - s) // NS + 1))

        @block.gpsimd
        def _(pool):
            def rstd_u(b, u):
                n = 2 * b + u
                pool.wait_ge(ukept, n + 1)
                pool.tensor_tensor(ur[:, u, :], kept(b, u)[:, 1, :], minus_half[:, 0:NB // 2], ALU.pow).then_inc(
                    urstd_done, 1)

            def rstd_x(b):
                for part in range(2):
                    four = slice(NB // 2 * part, NB // 2 * (part + 1))
                    if not (isinstance(b, int) and b == 0):
                        pool.wait_ge(g_done, 4 * b - 2 + 2 * part)
                    pool.wait_ge(xve_done, b + 1)
                    pool.tensor_tensor(xr[:, four], xve[:, four], minus_half[:, four], ALU.pow).then_inc(xrstd_done, 1)

            pool.memset(padded[:, :, :, :].rearrange("p a k f -> p (a k f)"), 0.0).then_inc(cleared, 1)
            pool.wait_ge(w_var_done, 1)
            pool.tensor_tensor(wrstd[:, :], wvar[:, :], minus_half[:, 0:J], ALU.pow).then_inc(w_rstd_done, 1)
            rstd_x(0)

            def pass1(i, c):
                b = NS * i + c
                if not is_first(i, c):
                    rstd_u(b - 1, UB)
                if not is_last(i, c, NS):
                    rstd_x(b + 1)
                rstd_u(b, UA)

            blocks(pool, pass1, NS)
            rstd_u(B - 1, UB)

            pool.wait_ge(bn1_step, BN1_STEPS)
            pool.tensor_tensor(btmp[:, 1, :], btmp[:, 0, :], minus_half[:, 0:J], ALU.pow).then_inc(bn1_pow, 1)
            pool.wait_ge(ukept, 2 * B)
            pool.tensor_tensor(gn1[:, :, 1, :], gn1[:, :, 1, :],
                               half[:, 0:1].unsqueeze(2).to_broadcast([P, B, NB]), ALU.pow).then_inc(root_done, 1)
            pool.wait_ge(bn2_step, J + 3)
            pool.tensor_tensor(btmp[:, 3, :], btmp[:, 2, :], minus_half[:, 0:J], ALU.pow).then_inc(bn2_pow, 1)

            def pass3(i, c):
                b = NS * i + c
                s = c % NS
                pool.wait_ge(y3_loaded[s], 16 * (i + c // NS + 1))
                pool.wait_ge(affine_done, b + 1)
                pool.tensor_tensor(ring_b[:, s, :], ring_b[:, s, :], ring_a[:, s, :], ALU.add).then_inc(v_done, 1)

            blocks(pool, pass3, NS)

        @block.scalar
        def _(act):
            act.wait_ge(const_loaded, 16 * N_CONST)
            act.wait_ge(cleared, 2)
            for g in range(P // CG):
                rows = slice(CG * g, CG * g + CG)
                act.activation(cw_sign[rows, :, :, rows],
                               cw[rows, :, :].rearrange("p k (i t) -> p k t i", t=TAPS), ACT.Sign).then_inc(cw_signed, 1)
            act.wait_ge(w_centred, J)
            for k in range(J):
                act.activation(cw_cent[:, k, :], cw_cent[:, k, :], ACT.Abs,
                               accum_out=wabs[:, k:k + 1]).then_inc(w_abs_done, 1)

            def normalise_x(i, c, k):
                s = c % NS
                if k % 2 == 0:
                    act.wait_ge(xnm_done, 2 * (NS * i + c) + k // 2 + 1)
                for n in (PER * k, PER * k + 1):
                    cols = slice(J * S * n, J * S * (n + 1))
                    last = act.activation(ring_b[:, s, cols], ring_a[:, s, cols], ACT.Identity,
                                          bias=xnm[:, n:n + 1], scale=xr[:, n:n + 1])
                last.then_inc(g_done, 1)

            def copy_turned(i, c, k):
                act.wait_ge(turned, 4 * (NS * i + c) + k + 1)
                act.activation(gT[:, k, :], bank_of(c, k), ACT.Copy).then_inc(gT_done, 1)

            def normalise_x1(i, c, k):
                b = NS * i + c
                s, u = c % NS, k // 2
                if k % 2 == 0:
                    act.wait_ge(unm_done, 2 * b + u + 1)
                if k == 0 and not is_first(i, c, NS):
                    act.wait_ge(y_stored[s], 16 * (i + c // NS))
                    act.wait_ge(ychan_done, b - 2)
                tile = ring_c[:, s, :].rearrange("p (j n s) -> p j n s", j=J, n=NB)
                for h in range(PER):
                    m = PER * (k % 2) + h
                    last = act.activation(
                        tile[:, :, PER * k + h, :],
                        bank_of(c, k)[:, J * S * h:J * S * (h + 1)].rearrange("p (j s) -> p j s", j=J),
                        ACT.Identity, bias=unm[:, u, m:m + 1], scale=ur[:, u, m:m + 1])
                last.then_inc(y_done, 1)

            act.wait_ge(x_loaded[0], 16)
            normalise_x(0, 0, 0)
            normalise_x(0, 0, 1)
            copy_turned(0, 0, 0)

            def pass1(i, c):
                before = not is_first(i, c)
                after = not is_last(i, c, NS)
                copy_turned(i, c, 1)
                if before:
                    normalise_x1(i, c - 1, 0)
                normalise_x(i, c, 2)
                copy_turned(i, c, 2)
                if before:
                    normalise_x1(i, c - 1, 1)
                normalise_x(i, c, 3)
                copy_turned(i, c, 3)
                if before:
                    normalise_x1(i, c - 1, 2)
                    normalise_x1(i, c - 1, 3)
                if after:
                    normalise_x(i, c + 1, 0)
                    normalise_x(i, c + 1, 1)
                    copy_turned(i, c + 1, 0)

            blocks(act, pass1, NS)
            for k in range(BANKS):
                normalise_x1((B - 1) // NS, (B - 1) % NS, k)

            def y2_slot(s):
                return ring_a[:, s, :] if s < NS else ring_b[:, s - NS, :]

            def take_sign(i, c, k):
                b = NS2 * i + c
                if k == 0:
                    act.wait_ge(y2_loaded[c % NS2], 16 * (i + c // NS2 + 1))
                if not is_first(i, c, 2):
                    act.wait_ge(conv_done, 4 * b - 7 + k)
                frame = padded[:, c % 2, k, :].rearrange("p (n a b) -> p n a b", n=NB, a=PAD)
                act.activation(frame[:, :, 1:1 + SIDE, 1:1 + SIDE],
                               y2_slot(c % NS2).rearrange("p (k n a b) -> p k n a b", k=J, n=NB, a=SIDE)[:, k],
                               ACT.Sign, bias=bn1_c[:, k, 1:2], scale=bn1_c[:, k, 0:1]).then_inc(signed, 1)

            def copy_h(i, c, k):
                b = NS2 * i + c
                act.wait_ge(conv_done, 4 * b + k + 1)
                if k == 0 and not is_first(i, c, NS2):
                    act.wait_ge(h_stored[c % NS2], 16 * (i + c // NS2))
                    act.wait_ge(h_counted, 4 * b - 12)
                act.activation(ring_h[:, c % NS2, BANK * k:BANK * (k + 1)], h_bank[4 * (c % 2) + k],
                               ACT.Copy).then_inc(h_copied, 1)

            act.wait_ge(bn1_in, 16)
            for k in range(J):
                take_sign(0, 0, k)

            def pass2(i, c):
                for k in range(J):
                    if not is_last(i, c, NS2):
                        take_sign(i, c + 1, k)
                    copy_h(i, c, k)

            blocks(act, pass2, NS2)

            def affine_h(i, c):
                b = NS * i + c
                s = c % NS
                act.wait_ge(h3_loaded[s], 16 * (i + c // NS + 1))
                if not is_first(i, c, 3):
                    act.wait_ge(res_done, b - 2)
                for j in range(J):
                    cols = slice(BANK * j, BANK * (j + 1))
                    last = act.activation(ring_b[:, s, cols], ring_h[:, s, cols], ACT.Identity,
                                          bias=bn2_q[:, j, 1:2], scale=bn2_q[:, j, 0:1])
                last.then_inc(affine_done, 1)

            def relu_v(i, c):
                b = NS * i + c
                s = c % NS
                act.wait_ge(v_done, b + 1)
                if not is_first(i, c, NS):
                    act.wait_ge(out_stored[s], 16 * (i + c // NS))
                act.activation(ring_c[:, s, :].rearrange("p (n j s) -> p j n s", n=NB, j=J),
                               ring_b[:, s, :].rearrange("p (j n s) -> p j n s", n=NB, j=J),
                               ACT.Relu).then_inc(relu_done, 1)

            act.wait_ge(bn2_in, 16)
            affine_h(0, 0)

            def pass3(i, c):
                if not is_last(i, c, NS):
                    affine_h(i, c + 1)
                relu_v(i, c)

            blocks(act, pass3, NS)

        @block.vector
        def _(dve):
            steps = [0]

            def step(ins, signal=prep, count=steps):
                count[0] += 1
                ins.then_inc(signal, 1)
                dve.wait_ge(signal, count[0])

            dve.memset(cw_sign[:, :, :, :].rearrange("p k t f -> p (k t f)"), 0.0).then_inc(cleared, 1)
            dve.memset(ones[:, :], 1.0)
            dve.memset(minus_half[:, :], -0.5)
            dve.memset(half[:, :], 0.5)
            dve.memset(mean_eps[:, 0, :], 0.0)
            dve.memset(mean_eps[:, 1, :], EPS)
            dve.memset(bias3[:, :], 0.0)
            step(dve.memset(W0T[:, :], 0.0))
            dve.wait_ge(const_loaded, 16 * N_CONST)

            step(dve.tensor_copy(identb[:, :], ident[:, :]))
            for n in range(3):
                step(dve.tensor_copy(bpart[:, n, :], brow[:, n, :]))
                if n < 2:
                    step(dve.tensor_tensor(brow[:, n + 1, :], brow[:, n, :], bpart[:, n, :], ALU.subtract))
                step(dve.tensor_copy(bias3[32 * n:32 * n + 1, :].rearrange("p (r f) -> p r f", f=S),
                                     bpart[:, n:n + 1, :].to_broadcast([1, BANK // S, S])))
            taken = CG * TAPS
            for k in range(J):
                step(dve.bn_stats(wtup[:, k, :], cw[:, k, :]))
                step(dve.bn_aggr(wagg[:, k, :], wtup[:, k, :]))
                dve.tensor_scalar(cw_cent[:, k, :], cw[:, k, :], wagg[:, k, 0:1], None,
                                  ALU.subtract).then_inc(w_centred, 1)
            dve.tensor_scalar(wvar[:, :], wagg[:, :, 1], taken / (taken - 1), None, ALU.mult).then_inc(w_var_done, 1)
            dve.wait_ge(w_rstd_done, 1)
            dve.wait_ge(w_abs_done, J)
            step(dve.tensor_scalar(scale_w[:, :], wabs[:, :], 1.0 / taken, None, ALU.mult))
            step(dve.tensor_tensor(scale_w[:, :], scale_w[:, :], wrstd[:, :], ALU.mult))
            step(dve.tensor_scalar(slope[:, 1, :], slope[:, 1, :], -1.0, 1.0, ALU.mult, ALU.add))
            dve.wait_ge(w0_summed, 1)
            for d in range(2):
                rows = slice(S * d, S * d + S)
                step(dve.tensor_copy(W0T[rows, rows].rearrange("p (o k) -> p k o", k=8),
                                     psW[rows, 0:S].rearrange("p (k o) -> p k o", k=8)))
            for k in range(J):
                dve.wait_ge(cw_turned, k + 1)
                step(dve.tensor_copy(conv_wT[:, k, :, :].rearrange("p t f -> p (t f)"),
                                     psX[:, 0:2, :].rearrange("p a f -> p (a f)").bitcast(BF16)[:, 0:TAPS * P]))

            def halves(tup, at):
                return tup.rearrange("p n (h s) -> p n h s", s=3)[:, :, :, at]

            def pairs(tile):
                return tile.rearrange("p (n h) -> p n h", h=2)

            def x_stat(i, c, n):
                if n == 0:
                    dve.wait_ge(x_loaded[c % NS], 16 * (i + c // NS + 1))
                last = dve.bn_stats(xs[:, n, :], ring_a[:, c % NS, J * S * n:J * S * (n + 1)])
                if n == NB - 1:
                    last.then_inc(xbn_done, 1)

            def x_sum(b):
                dve.wait_ge(xbn_done, b + 1)
                dve.tensor_tensor(xsum[:, :], xs[:, :, 1], xs[:, :, 4], ALU.add).then_inc(xsum_done, 1)

            def x_deviation(b):
                dve.wait_ge(xmean_done, b + 1)
                dve.tensor_tensor(pairs(xdev[:, 0, :]), halves(xs[:, :, :], 1),
                                  x_mean.unsqueeze(2).to_broadcast([P, NB, 2]), ALU.subtract).then_inc(xdev_step, 1)

            def x_square(b):
                dve.wait_ge(xdev_step, 3 * b + 1)
                dve.tensor_tensor(xdev[:, 1, :], xdev[:, 0, :], xdev[:, 0, :], ALU.mult).then_inc(xdev_step, 1)

            def x_moment(b):
                dve.wait_ge(xdev_step, 3 * b + 2)
                dve.scalar_tensor_tensor(out=pairs(xdev[:, 2, :]), in0=halves(xs[:, :, :], 2), scalar=2.0 / (J * S),
                                         in1=pairs(xdev[:, 1, :]), op0=ALU.mult, op1=ALU.add).then_inc(xdev_step, 1)

            def x_moments(b):
                dve.wait_ge(xdev_step, 3 * b + 3)
                d = pairs(xdev[:, 2, :])
                dve.tensor_tensor(xdevs[:, :], d[:, :, 0], d[:, :, 1], ALU.add).then_inc(xdev_done, 1)

            def x_variance(b):
                dve.wait_ge(xvar_done, b + 1)
                dve.tensor_scalar(xve[:, :], x_var, EPS, None, ALU.add).then_inc(xve_done, 1)

            def x_addend(b, part):
                four = slice(NB // 2 * part, NB // 2 * (part + 1))
                dve.wait_ge(xrstd_done, 2 * b + part + 1)
                dve.scalar_tensor_tensor(out=xnm[:, four], in0=x_mean[:, four], scalar=-1.0, in1=xr[:, four],
                                         op0=ALU.mult, op1=ALU.mult).then_inc(xnm_done, 1)

            def u_stat(i, c, k, h):
                if h == 0:
                    dve.wait_ge(x1_done, 4 * (NS * i + c) + k + 1)
                last = dve.bn_stats(us[:, k // 2, PER * (k % 2) + h, :], bank_of(c, k)[:, J * S * h:J * S * (h + 1)])
                if k % 2 and h:
                    last.then_inc(ubn_done, 1)

            def u_sum(b, u):
                dve.wait_ge(ubn_done, 2 * b + u + 1)
                dve.tensor_tensor(usum[:, u, :], us[:, u, :, 1], us[:, u, :, 4], ALU.add).then_inc(usum_done, 1)

            def u_deviation(b, u):
                dve.wait_ge(umean_done, 2 * b + u + 1)
                dve.tensor_tensor(pairs(udev[:, u, 0, :]), halves(us[:, u, :, :], 1),
                                  u_mean[u].unsqueeze(2).to_broadcast([P, NB // 2, 2]),
                                  ALU.subtract).then_inc(udev_step, 1)

            def u_square(b, u):
                dve.wait_ge(udev_step, 6 * b + 3 * u + 1)
                dve.tensor_tensor(udev[:, u, 1, :], udev[:, u, 0, :], udev[:, u, 0, :], ALU.mult).then_inc(udev_step, 1)

            def u_moment(b, u):
                dve.wait_ge(udev_step, 6 * b + 3 * u + 2)
                dve.scalar_tensor_tensor(out=pairs(udev[:, u, 2, :]), in0=halves(us[:, u, :, :], 2),
                                         scalar=2.0 / (J * S), in1=pairs(udev[:, u, 1, :]),
                                         op0=ALU.mult, op1=ALU.add).then_inc(udev_step, 1)

            def u_moments(b, u):
                dve.wait_ge(udev_step, 6 * b + 3 * u + 3)
                d = pairs(udev[:, u, 2, :])
                dve.tensor_tensor(udevs[:, u, :], d[:, :, 0], d[:, :, 1], ALU.add).then_inc(udev_done, 1)

            def u_keep(b, u):
                dve.wait_ge(uvar_done, 2 * b + u + 1)
                both = psS[:, 16 + 8 * u:24 + 8 * u].rearrange("p (m n) -> p m n", m=2)
                dve.tensor_tensor(kept(b, u), both, mean_eps[:, :, :], ALU.add).then_inc(ukept, 1)

            def u_addend(b, u):
                dve.wait_ge(urstd_done, 2 * b + u + 1)
                dve.scalar_tensor_tensor(out=unm[:, u, :], in0=u_mean[u], scalar=-1.0, in1=ur[:, u, :],
                                         op0=ALU.mult, op1=ALU.mult).then_inc(unm_done, 1)

            def count_y(i, c, j):
                b = NS * i + c
                if j == 0:
                    dve.wait_ge(y_done, 4 * b + 4)
                to = y_tuples[:, b, j, :] if isinstance(b, int) else y_tuples[:, bass.ds(b, 1), j, :].rearrange(
                    "p a s -> p (a s)")
                last = dve.bn_stats(to, ring_c[:, c % NS, BANK * j:BANK * (j + 1)])
                if j == J - 1:
                    last.then_inc(ychan_done, 1)

            for n in range(NB):
                x_stat(0, 0, n)
            x_sum(0)
            x_deviation(0)
            x_square(0)
            x_moment(0)
            x_moments(0)
            x_variance(0)
            x_addend(0, 0)
            x_addend(0, 1)

            def pass1(i, c):
                b = NS * i + c
                before = not is_first(i, c)
                twice = not is_first(i, c, 2)
                after = not is_last(i, c, NS)
                if before:
                    u_stat(i, c - 1, 3, 0)
                    u_addend(b - 1, UA)
                    u_stat(i, c - 1, 3, 1)
                if after:
                    x_stat(i, c + 1, 0)
                if before:
                    u_sum(b - 1, UB)
                if after:
                    for n in range(1, 6):
                        x_stat(i, c + 1, n)
                if before:
                    u_deviation(b - 1, UB)
                if after:
                    x_stat(i, c + 1, 6)
                if before:
                    u_square(b - 1, UB)
                if after:
                    x_stat(i, c + 1, 7)
                if before:
                    u_moment(b - 1, UB)
                if after:
                    x_sum(b + 1)
                u_stat(i, c, 0, 0)
                if before:
                    u_moments(b - 1, UB)
                u_stat(i, c, 0, 1)
                if after:
                    x_deviation(b + 1)
                if before:
                    u_keep(b - 1, UB)
                if after:
                    x_square(b + 1)
                    x_moment(b + 1)
                    x_moments(b + 1)
                u_stat(i, c, 1, 0)
                if before:
                    u_addend(b - 1, UB)
                if after:
                    x_variance(b + 1)
                u_stat(i, c, 1, 1)
                u_sum(b, UA)
                if twice:
                    count_y(i, c - 2, 2)
                if after:
                    x_addend(b + 1, 0)
                u_deviation(b, UA)
                if twice:
                    count_y(i, c - 2, 3)
                u_square(b, UA)
                u_stat(i, c, 2, 0)
                if after:
                    x_addend(b + 1, 1)
                u_moment(b, UA)
                u_stat(i, c, 2, 1)
                u_moments(b, UA)
                if before:
                    count_y(i, c - 1, 0)
                u_keep(b, UA)
                if before:
                    count_y(i, c - 1, 1)

            blocks(dve, pass1, NS)
            end_i, end_c = (B - 1) // NS, (B - 1) % NS
            u_stat(end_i, end_c, 3, 0)
            u_addend(B - 1, UA)
            u_stat(end_i, end_c, 3, 1)
            for part in (u_sum, u_deviation, u_square, u_moment, u_moments, u_keep, u_addend):
                part(B - 1, UB)
            for j in (2, 3):
                count_y((B - 2) // NS, (B - 2) % NS, j)
            for j in range(J):
                count_y(end_i, end_c, j)

            done = [0]
            dve.wait_ge(ychan_done, B)
            for j in range(J):
                step(dve.bn_aggr(bagg[:, j, :], y_tuples[:, :, j, :]), bn1_step, done)
            step(dve.tensor_scalar(btmp[:, 0, :], bagg[:, :, 1], EPS, None, ALU.add), bn1_step, done)
            dve.wait_ge(bn1_pow, 1)
            step(dve.tensor_tensor(bn1_q[:, :, 0], gb1[:, 0, :], btmp[:, 1, :], ALU.mult), bn1_step, done)
            step(dve.tensor_tensor(btmp[:, 2, :], bagg[:, :, 0], bn1_q[:, :, 0], ALU.mult), bn1_step, done)
            dve.tensor_tensor(bn1_q[:, :, 1], gb1[:, 1, :], btmp[:, 2, :], ALU.subtract).then_inc(bn1_ready, 1)

            def pass2(i, c):
                b = NS2 * i + c
                for k in range(J):
                    dve.wait_ge(h_copied, 4 * b + k + 1)
                    to = h_tuples[:, b, k, :] if isinstance(b, int) else h_tuples[:, bass.ds(b, 1), k, :].rearrange(
                        "p a s -> p (a s)")
                    dve.bn_stats(to, ring_h[:, c % NS2, BANK * k:BANK * (k + 1)]).then_inc(h_counted, 1)

            blocks(dve, pass2, NS2)

            done = [0]
            dve.wait_ge(h_counted, 4 * B)
            for k in range(J):
                step(dve.bn_aggr(bagg[:, k, :], h_tuples[:, :, k, :]), bn2_step, done)
            step(dve.tensor_tensor(btmp[:, 0, :], bagg[:, :, 1], scale_w[:, :], ALU.mult), bn2_step, done)
            step(dve.tensor_tensor(btmp[:, 1, :], btmp[:, 0, :], scale_w[:, :], ALU.mult), bn2_step, done)
            step(dve.tensor_scalar(btmp[:, 2, :], btmp[:, 1, :], EPS, None, ALU.add), bn2_step, done)
            dve.wait_ge(bn2_pow, 1)
            step(dve.tensor_tensor(btmp[:, 0, :], gb2[:, 0, :], scale_w[:, :], ALU.mult), bn2_step, done)
            step(dve.tensor_tensor(bn2_c[:, :, 0], btmp[:, 0, :], btmp[:, 3, :], ALU.mult), bn2_step, done)
            step(dve.tensor_tensor(btmp[:, 1, :], bagg[:, :, 0], bn2_c[:, :, 0], ALU.mult), bn2_step, done)
            dve.tensor_tensor(bn2_c[:, :, 1], gb2[:, 1, :], btmp[:, 1, :], ALU.subtract).then_inc(bn2_ready, 1)
            dve.wait_ge(root_done, 1)

            def pass3(i, c):
                b = NS * i + c
                s = c % NS
                stats = gn1[:, b, :, :] if isinstance(b, int) else gn1[:, bass.ds(b, 1), :, :].rearrange(
                    "p a m n -> p (a m) n")
                if not is_first(i, c):
                    dve.wait_ge(x1_rebuilt, b)
                dve.tensor_copy(gnb[:, :, :], stats).then_inc(gn_copied, 1)
                dve.wait_ge(gn_copied, b + 1)
                dve.wait_ge(v_done, b + 1)
                y = ring_a[:, s, :].rearrange("p (j n s) -> p j n s", j=J, n=NB)
                for n in range(NB):
                    last = dve.tensor_scalar(y[:, :, n, :], y[:, :, n, :], gnb[:, 1, n:n + 1], gnb[:, 0, n:n + 1],
                                             ALU.mult, ALU.add)
                last.then_inc(x1_rebuilt, 1)
                dve.wait_ge(x1_rebuilt, b + 1)
                dve.wait_ge(relu_done, b + 1)
                for j in range(J):
                    cols = slice(BANK * j, BANK * (j + 1))
                    last = dve.scalar_tensor_tensor(out=ring_b[:, s, cols], in0=ring_b[:, s, cols],
                                                    scalar=slope[:, 0, j:j + 1], in1=ring_a[:, s, cols],
                                                    op0=ALU.mult, op1=ALU.add)
                last.then_inc(z_done, 1)
                dve.wait_ge(z_done, b + 1)
                res = ring_c[:, s, :].rearrange("p (n j s) -> p j n s", n=NB, j=J)
                for j in range(J):
                    last = dve.scalar_tensor_tensor(
                        out=res[:, j], in0=res[:, j], scalar=slope[:, 1, j:j + 1],
                        in1=ring_b[:, s, BANK * j:BANK * (j + 1)].rearrange("p (n s) -> p n s", n=NB),
                        op0=ALU.mult, op1=ALU.add)
                last.then_inc(res_done, 1)

            blocks(dve, pass3, NS)

        @block.tensor
        def _(pe):
            def turn(i, c, k):
                b = NS * i + c
                s = c % NS
                pe.wait_ge(g_done, 4 * b + k + 1)
                if not (is_first(i, c) or (is_first(i, c, 2) and k < RING - BANKS)):
                    pe.wait_ge(y_done, 4 * b + k + 1 - RING)
                for m in range(4):
                    last = pe.transpose(bank_of(c, k)[:, P * m:P * (m + 1)],
                                        ring_b[:, s, BANK * k + P * m:BANK * k + P * (m + 1)], ident[:, :])
                last.then_inc(turned, 1)

            def product(c, k, m):
                return pe.matmul(bank_of(c, k)[:, P * m:P * (m + 1)], gT[:, k, P * m:P * (m + 1)], W0T[:, :],
                                 start=False, stop=(m == 3))

            def begin_bank(i, c, k):
                pe.wait_ge(gT_done, 4 * (NS * i + c) + k + 1)
                pe.matmul(bank_of(c, k), ident[:, :], ring_a[:, c % NS, BANK * k:BANK * (k + 1)],
                          start=True, stop=False)
                pe.matmul(bank_of(c, k), ones[:, :], bias3[:, :], start=False, stop=False)
                product(c, k, 0)
                product(c, k, 1)

            def end_bank(c, k):
                product(c, k, 2)
                product(c, k, 3).then_inc(x1_done, 1)

            def x_mean_of(b):
                pe.wait_ge(xsum_done, b + 1)
                pe.matmul(x_mean, gavg[:, :], xsum[:, :], start=True, stop=True).then_inc(xmean_done, 1)

            def x_var_of(b):
                pe.wait_ge(xdev_done, b + 1)
                pe.matmul(x_var, gavg[:, :], xdevs[:, :], start=True, stop=True).then_inc(xvar_done, 1)

            def u_mean_of(b, u):
                pe.wait_ge(usum_done, 2 * b + u + 1)
                if not (isinstance(b, int) and b == 0 and u == UA):
                    pe.wait_ge(unm_done, 2 * b + u)
                pe.matmul(u_mean[u], gavg[:, :], usum[:, u, :], start=True, stop=True).then_inc(umean_done, 1)

            def u_var_of(b, u):
                pe.wait_ge(udev_done, 2 * b + u + 1)
                pe.matmul(u_var[u], gavg[:, :], udevs[:, u, :], start=True, stop=True).then_inc(uvar_done, 1)

            pe.wait_ge(const_loaded, 16 * N_CONST)
            for k in range(8):
                last = pe.matmul(psW[:, 8 * k:8 * k + 8], clif[:, k, :], w0_sb[:, :], start=True, stop=True)
            last.then_inc(w0_summed, 1)
            pe.wait_ge(cw_signed, P // CG)
            turned_w = psX[:, 0:2, :].rearrange("p a f -> p (a f)").bitcast(BF16)
            first_copy = 23
            for k in range(J):
                pe.wait_ge(prep, first_copy + k)
                for t in range(TAPS):
                    last = pe.transpose(turned_w[:, P * t:P * (t + 1)], cw_sign[:, k, t, :], identb[:, :])
                last.then_inc(cw_turned, 1)

            x_mean_of(0)
            x_var_of(0)
            turn(0, 0, 0)
            pe.wait_ge(prep, first_copy + J)

            def pass1(i, c):
                b = NS * i + c
                before = not is_first(i, c)
                after = not is_last(i, c, NS)
                turn(i, c, 1)
                begin_bank(i, c, 0)
                end_bank(c, 0)
                if before:
                    u_mean_of(b - 1, UB)
                turn(i, c, 2)
                begin_bank(i, c, 1)
                if after:
                    x_mean_of(b + 1)
                if before:
                    u_var_of(b - 1, UB)
                end_bank(c, 1)
                if after:
                    x_var_of(b + 1)
                turn(i, c, 3)
                begin_bank(i, c, 2)
                u_mean_of(b, UA)
                end_bank(c, 2)
                begin_bank(i, c, 3)
                u_var_of(b, UA)
                if after:
                    turn(i, c + 1, 0)
                end_bank(c, 3)

            blocks(pe, pass1, NS)
            u_mean_of(B - 1, UB)
            u_var_of(B - 1, UB)

            pe.wait_ge(cleared, 2)
            pe.wait_ge(y_done, 4 * B)
            pe.wait_ge(unm_done, 2 * B)

            def pass2(i, c):
                b = NS2 * i + c
                for k in range(J):
                    pe.wait_ge(signed, 4 * b + k + 1)
                    if not is_first(i, c, 2):
                        pe.wait_ge(h_copied, 4 * b - 7 + k)
                    frame = padded[:, c % 2, k, :].rearrange("p (n a b) -> p n a b", n=NB, a=PAD)
                    for t in range(TAPS):
                        dy, dx = t // 3, t % 3
                        last = pe.matmul(h_bank[4 * (c % 2) + k], conv_wT[:, k, t, :],
                                         frame[:, :, dy:dy + SIDE, dx:dx + SIDE],
                                         start=(t == 0), stop=(t == TAPS - 1))
                    last.then_inc(conv_done, 1)

            blocks(pe, pass2, NS2)


_NAMES = ["x", "L0_conv_weight", "L0_conv_bias", "L1_conv_conv_w", "L1_conv_bn1_gamma", "L1_conv_bn1_beta",
          "L1_conv_bn2_gamma", "L1_conv_bn2_beta", "L1_conv_prelu_a"]


def constants():
    group = np.kron(np.eye(P // 4), np.full((4, 4), 1 / 8)).astype(np.float32)
    sel = np.einsum("kpq,ij->ipkjq", clifford_terms(), np.eye(8, dtype=np.float32)).reshape(S, 8, S)
    return {"identity": np.eye(P, dtype=np.float32), "group_average": group,
            "algebra": np.ascontiguousarray(np.concatenate([sel, sel], axis=2))}


def kernel(**inputs):
    import concourse.bacc as bacc
    from concourse.bass_utils import run_bass_kernel_spmd

    nc = bacc.Bacc("TRN2", target_bir_lowering=False, num_devices=1)
    arrays = {f"in_{n}": np.ascontiguousarray(inputs[n]) for n in _NAMES}
    arrays.update(constants())
    args = [nc.dram_tensor(n, a.shape, mybir.dt.from_np(a.dtype), kind="ExternalInput").ap()
            for n, a in arrays.items()]
    out = nc.dram_tensor("out", inputs["x"].shape, F32, kind="ExternalOutput").ap()
    two_layer_kernel(nc, *args, out)
    r = run_bass_kernel_spmd(nc, [arrays], core_ids=[0])
    return r.results[0]["out"]
```
